# Optimizing a Trainium2 kernel written in Bass

```python
import numpy as np
import jax
import jax.numpy as jnp

def _softmax(x, axis=-1):
    return jax.nn.softmax(x, axis=axis)
def _gelu(x):
    return jax.nn.gelu(x, approximate=True)
def _silu(x):
    return jax.nn.silu(x)
def _sigmoid(x):
    return jax.nn.sigmoid(x)
def _layernorm(x, axis=-1, eps=1e-5):
    m = jnp.mean(x, axis=axis, keepdims=True)
    v = jnp.var(x, axis=axis, keepdims=True)
    return (x - m) / jnp.sqrt(v + eps)
def _scatter_add(tgt, idx, src, axis=0):
    return tgt.at[idx].add(src)
def _segment_sum(src, seg, n):
    return jax.ops.segment_sum(src, seg, n)

kernel_name = 'mk_adj_resnorm_d4_adj_256_8370fe'

def setup_inputs(seed: int = 0):
    np.random.seed(seed)
    _w = jnp.asarray
    def _rec_inputs():
        import jax
        import jax.numpy as jnp
        _gk = jax.random.key(seed)
        x = -0.0002928 + 1 * jax.random.normal(jax.random.fold_in(_gk, 1), (32, 512, 256), jnp.float32)
        _a = jax.random.bernoulli(jax.random.fold_in(_gk, 2), 0.03125, (512, 512))
        _a = jnp.logical_or(_a, jnp.swapaxes(_a, -1, -2))
        _a = jnp.logical_or(_a, jnp.eye(512, dtype=bool))
        adj = _a.astype(jnp.int32)
        return x, adj
    x, adj = _rec_inputs()
    def _L0_gnn_setup():
        import jax, jax.numpy as jnp
        import numpy as np
        ALPHA = 0.2
        NEG_INF = -9000000000000000.0

        def _gat(inp, adj_mask, W, a):
            h = jnp.matmul(inp, W)
            F_ = h.shape[-1]
            f1 = jnp.matmul(h, a[:F_, 0])
            f2 = jnp.matmul(h, a[F_:, 0])
            e = jax.nn.leaky_relu(f1[:, :, None] + f2[:, None, :], ALPHA)
            if adj_mask is not None:
                e = jnp.where(adj_mask[None, :, :] > 0, e, NEG_INF)
            att = jax.nn.softmax(e, axis=2)
            h_prime = jnp.einsum('bij,bjf->bif', att, h)
            return jax.nn.elu(h_prime)
        key = jax.random.key(seed)
        ks = jax.random.split(key, 10)
        B, N, Fin, H, O = (16, 1024, 256, 512, 256)

        def xavier(k, shape):
            fan_in, fan_out = (shape[0], shape[-1])
            bound = 1.414 * np.sqrt(6.0 / (fan_in + fan_out))
            return jax.random.uniform(k, shape, jnp.float32, -bound, bound)
        return {'x': jax.random.normal(ks[0], (B, N, Fin), jnp.float32), 'adj': jax.random.randint(ks[1], (N, N), 0, 2, jnp.int32), 'mlp1_w': xavier(ks[2], (Fin, H)), 'mlp1_b': jnp.zeros((H,), jnp.float32), 'mlp2_w': xavier(ks[3], (H, O)), 'mlp2_b': jnp.zeros((O,), jnp.float32), 'W_fc': xavier(ks[4], (H, H)), 'a_fc': xavier(ks[5], (2 * H, 1)), 'W_hand': xavier(ks[6], (O, O)), 'a_hand': xavier(ks[7], (2 * O, 1))}
    _L0_gnn_all = _L0_gnn_setup()
    _L0_gnn_in = {k: v for k, v in _L0_gnn_all.items() if k in ('mlp1_w', 'mlp1_b', 'mlp2_w', 'mlp2_b', 'W_fc', 'a_fc', 'W_hand', 'a_hand', )}
    del _L0_gnn_all

    def _L1_gnn_setup():
        import jax, jax.numpy as jnp
        import numpy as np
        ALPHA = 0.2
        EPS = 1e-06
        key = jax.random.key(seed)
        ks = jax.random.split(key, 8)
        B, N, D, H = (2, 2048, 256, 8)
        dh = D // H
        x = jax.random.normal(ks[0], (B, N, D), dtype=jnp.float32)
        adj = jax.random.randint(ks[1], (N, N), 0, 2, dtype=jnp.int32)
        adj = jnp.maximum(adj, jnp.eye(N, dtype=jnp.int32))
        p = jax.random.uniform(ks[2], (B, N, N), dtype=jnp.float32)
        prior = p / jnp.sum(p, axis=-1, keepdims=True)
        W = jax.random.normal(ks[3], (H, D, dh), dtype=jnp.float32) * (1.0 / np.sqrt(D))
        a_src = jax.random.normal(ks[4], (H, dh), dtype=jnp.float32) * (1.0 / np.sqrt(dh))
        a_dst = jax.random.normal(ks[5], (H, dh), dtype=jnp.float32) * (1.0 / np.sqrt(dh))
        beta_tilde = jnp.ones((), dtype=jnp.float32)
        W_out = jax.random.normal(ks[6], (D, D), dtype=jnp.float32) * (1.0 / np.sqrt(D))
        return {'x': x, 'adj': adj, 'prior': prior, 'W': W, 'a_src': a_src, 'a_dst': a_dst, 'beta_tilde': beta_tilde, 'W_out': W_out}
    _L1_gnn_all = _L1_gnn_setup()
    _L1_gnn_in = {k: v for k, v in _L1_gnn_all.items() if k in ('W', 'a_src', 'a_dst', 'beta_tilde', 'W_out', )}
    del _L1_gnn_all

    def _L2_gnn_setup():
        import jax, jax.numpy as jnp
        import numpy as np
        ALPHA = 0.2
        MASK_VAL = -9000000000000000.0
        key = jax.random.key(seed)
        k1, k2, k3, k4 = jax.random.split(key, 4)
        B, N, F = (8, 1024, 256)
        H, OUT = (4, 256)
        hs = OUT // H
        x = jax.random.normal(k1, (B, N, F), dtype=jnp.float32)
        adj = jax.random.randint(k2, (N, N), 0, 2, dtype=jnp.int32)
        wb = float(np.sqrt(6.0 / (F + hs)))
        ab = float(np.sqrt(6.0 / (H + 2 * hs)))
        W = jax.random.uniform(k3, (H, F, hs), dtype=jnp.float32, minval=-wb, maxval=wb)
        a = jax.random.uniform(k4, (H, 2 * hs), dtype=jnp.float32, minval=-ab, maxval=ab)
        return {'x': x, 'adj': adj, 'W': W, 'a': a}
    _L2_gnn_all = _L2_gnn_setup()
    _L2_gnn_in = {k: v for k, v in _L2_gnn_all.items() if k in ('W', 'a', )}
    del _L2_gnn_all

    def _L3_gnn_setup():
        import jax, jax.numpy as jnp
        import numpy as np
        IN_DIM = 256
        OUT_DIM = 64
        NUM_HEADS = 4
        ALPHA = 0.2
        NEG_INF = -9000000000000000.0
        key = jax.random.key(seed)
        k1, k2, k3, k4 = jax.random.split(key, 4)
        B, N = (4, 2048)
        h = jax.random.normal(k1, (B, N, IN_DIM), dtype=jnp.float32)
        adj = jax.random.randint(k2, (N, N), 0, 2, dtype=jnp.int32)
        W = jax.random.normal(k3, (IN_DIM, NUM_HEADS * OUT_DIM), dtype=jnp.float32) * (1.0 / np.sqrt(IN_DIM))
        a = jax.random.normal(k4, (2 * OUT_DIM,), dtype=jnp.float32) * (1.0 / np.sqrt(2 * OUT_DIM))
        return {'h': h, 'adj': adj, 'W': W, 'a': a}
    _L3_gnn_all = _L3_gnn_setup()
    _L3_gnn_in = {k: v for k, v in _L3_gnn_all.items() if k in ('W', 'a', )}
    del _L3_gnn_all

    return {
        "x": x,
        "adj": adj,
        "L0_gnn_mlp1_w": _L0_gnn_in["mlp1_w"],
        "L0_gnn_mlp1_b": _L0_gnn_in["mlp1_b"],
        "L0_gnn_mlp2_w": _L0_gnn_in["mlp2_w"],
        "L0_gnn_mlp2_b": _L0_gnn_in["mlp2_b"],
        "L0_gnn_W_fc": _L0_gnn_in["W_fc"],
        "L0_gnn_a_fc": _L0_gnn_in["a_fc"],
        "L0_gnn_W_hand": _L0_gnn_in["W_hand"],
        "L0_gnn_a_hand": _L0_gnn_in["a_hand"],
        "L1_gnn_W": _L1_gnn_in["W"],
        "L1_gnn_a_src": _L1_gnn_in["a_src"],
        "L1_gnn_a_dst": _L1_gnn_in["a_dst"],
        "L1_gnn_beta_tilde": _L1_gnn_in["beta_tilde"],
        "L1_gnn_W_out": _L1_gnn_in["W_out"],
        "L2_gnn_W": _L2_gnn_in["W"],
        "L2_gnn_a": _L2_gnn_in["a"],
        "L3_gnn_W": _L3_gnn_in["W"],
        "L3_gnn_a": _L3_gnn_in["a"],
    }

def reference(x, adj, L0_gnn_mlp1_w, L0_gnn_mlp1_b, L0_gnn_mlp2_w, L0_gnn_mlp2_b, L0_gnn_W_fc, L0_gnn_a_fc, L0_gnn_W_hand, L0_gnn_a_hand, L1_gnn_W, L1_gnn_a_src, L1_gnn_a_dst, L1_gnn_beta_tilde, L1_gnn_W_out, L2_gnn_W, L2_gnn_a, L3_gnn_W, L3_gnn_a):
    import jax
    import jax.numpy as jnp
    def _L0_gnn_ref(x, adj, mlp1_w, mlp1_b, mlp2_w, mlp2_b, W_fc, a_fc, W_hand, a_hand):
        import jax, jax.numpy as jnp
        import numpy as np
        ALPHA = 0.2
        NEG_INF = -9000000000000000.0

        def _gat(inp, adj_mask, W, a):
            h = jnp.matmul(inp, W)
            F_ = h.shape[-1]
            f1 = jnp.matmul(h, a[:F_, 0])
            f2 = jnp.matmul(h, a[F_:, 0])
            e = jax.nn.leaky_relu(f1[:, :, None] + f2[:, None, :], ALPHA)
            if adj_mask is not None:
                e = jnp.where(adj_mask[None, :, :] > 0, e, NEG_INF)
            att = jax.nn.softmax(e, axis=2)
            h_prime = jnp.einsum('bij,bjf->bif', att, h)
            return jax.nn.elu(h_prime)
        out = jax.nn.relu(jnp.matmul(x, mlp1_w) + mlp1_b)
        residual = out
        out = _gat(jax.nn.relu(out), None, W_fc, a_fc)
        out = jax.nn.elu(out) + residual
        out = jax.nn.relu(jnp.matmul(out, mlp2_w) + mlp2_b)
        residual = out
        out = _gat(jax.nn.relu(out), adj, W_hand, a_hand)
        out = jax.nn.elu(out) + residual
        return jax.nn.relu(out)

    def _L1_gnn_ref(x, adj, prior, W, a_src, a_dst, beta_tilde, W_out):
        import jax, jax.numpy as jnp
        import numpy as np
        ALPHA = 0.2
        EPS = 1e-06
        B, N, D = x.shape
        x_proj = jnp.einsum('bnd,hdf->bhnf', x, W)
        e_src = jnp.einsum('bhnf,hf->bhn', x_proj, a_src)
        e_dst = jnp.einsum('bhnf,hf->bhn', x_proj, a_dst)
        e = jax.nn.leaky_relu(e_src[..., :, None] + e_dst[..., None, :], ALPHA)
        beta = jax.nn.softplus(beta_tilde)
        e = e + (beta * jnp.log(prior + EPS))[:, None, :, :]
        neg_inf = jnp.finfo(e.dtype).min
        e = jnp.where(adj[None, None, :, :] > 0, e, neg_inf)
        attn = jax.nn.softmax(e, axis=-1)
        h = jnp.einsum('bhij,bhjf->bhif', attn, x_proj)
        h = h.transpose(0, 2, 1, 3).reshape(B, N, D)
        return h @ W_out.T

    def _L2_gnn_ref(x, adj, W, a):
        import jax, jax.numpy as jnp
        import numpy as np
        ALPHA = 0.2
        MASK_VAL = -9000000000000000.0
        B, N, _ = x.shape
        H, _, hs = W.shape
        Wh = jnp.einsum('bnf,hfd->bhnd', x, W)
        a1, a2 = (a[:, :hs], a[:, hs:])
        ei = jnp.einsum('bhnd,hd->bhn', Wh, a1)
        ej = jnp.einsum('bhnd,hd->bhn', Wh, a2)
        e = ei[:, :, :, None] + ej[:, :, None, :]
        e = jnp.where(e > 0, e, ALPHA * e)
        e = jnp.where(adj[None, None] > 0, e, MASK_VAL)
        att = jax.nn.softmax(e, axis=-1)
        h = jnp.einsum('bhij,bhjd->bhid', att, Wh)
        h = h.transpose(0, 2, 1, 3).reshape(B, N, H * hs)
        return jax.nn.elu(h)

    def _L3_gnn_ref(h, adj, W, a):
        import jax, jax.numpy as jnp
        import numpy as np
        IN_DIM = 256
        OUT_DIM = 64
        NUM_HEADS = 4
        ALPHA = 0.2
        NEG_INF = -9000000000000000.0
        B, N, _ = h.shape
        H, D = (NUM_HEADS, OUT_DIM)
        q = (h @ W).reshape(B, N, H, D)
        a_src, a_dst = (a[:D], a[D:])
        e_src = jnp.einsum('bnhd,d->bnh', q, a_src)
        e_dst = jnp.einsum('bnhd,d->bnh', q, a_dst)
        e = e_src[:, :, None, :] + e_dst[:, None, :, :]
        e = jnp.where(e >= 0, e, ALPHA * e)
        mask = (adj > 0)[None, :, :, None]
        e = jnp.where(mask, e, NEG_INF)
        attn = jax.nn.softmax(e, axis=2)
        h_prime = jnp.einsum('bijh,bjhd->bihd', attn, q)
        return jax.nn.elu(h_prime.reshape(B, N, H * D))

    x = _layernorm(x + _L0_gnn_ref(x, adj, L0_gnn_mlp1_w, L0_gnn_mlp1_b, L0_gnn_mlp2_w, L0_gnn_mlp2_b, L0_gnn_W_fc, L0_gnn_a_fc, L0_gnn_W_hand, L0_gnn_a_hand), axis=-1)
    x = _layernorm(x + _L1_gnn_ref(x, adj, adj[None], L1_gnn_W, L1_gnn_a_src, L1_gnn_a_dst, L1_gnn_beta_tilde, L1_gnn_W_out), axis=-1)
    x = _layernorm(x + _L2_gnn_ref(x, adj, L2_gnn_W, L2_gnn_a), axis=-1)
    x = _layernorm(x + _L3_gnn_ref(x, adj, L3_gnn_W, L3_gnn_a), axis=-1)
    return x


_drawn_inputs = setup_inputs


def setup_inputs(seed=0):
    import zlib

    import numpy as np

    out = dict(_drawn_inputs(seed))
    spreads = {'L0_gnn_mlp1_b': (0.0, 0.1), 'L0_gnn_mlp2_b': (0.0, 0.1)}
    factors = {'L1_gnn_a_src': 3.089, 'L3_gnn_a': 3.522}
    for name, (base, spread) in spreads.items():
        noise = np.random.default_rng([zlib.crc32(name.encode()), seed]).standard_normal(out[name].shape)
        drawn = base * np.exp(spread * noise) if base else spread * noise
        out[name] = jnp.asarray(drawn.astype(out[name].dtype))
    for name, factor in factors.items():
        out[name] = (out[name] * factor).astype(out[name].dtype)
    return out
```

```python
from contextlib import ExitStack

import concourse.bass as bass
from concourse import mybir

ALU = mybir.AluOpType
ACT = mybir.ActivationFunctionType
AX = mybir.AxisListType
F32 = mybir.dt.float32
F32R = mybir.dt.float32r
BF16 = mybir.dt.bfloat16
I32 = mybir.dt.int32

P = 128
STREAMS = 2
BANKS = 8
EPS_LN = 1e-5
EPS_PRIOR = 1e-6
V_SETUP = 58
SLOPE = 0.2
Z_MIN = -75.0

HEADS = {0: 1, 1: 1, 2: 8, 3: 4, 4: 4}
WIDE = (0, 1)
MULTI = (2, 3, 4)


class Signal:

    def __init__(self, ctx, nc, name, per):
        self.sem = ctx.enter_context(nc.semaphore(name))
        self.per = per

    def upto(self, it, k):
        return it * self.per + k


def tensor_jobs():
    both = range(STREAMS)
    for s in both:
        for k in range(2):
            yield ("xT", s, 0, k)
    for s in both:
        for c in range(4):
            yield ("mlp1", s, c)
    for s in both:
        yield ("rows", s, 0)
    for s in both:
        for t in range(4):
            for half in range(2):
                yield ("h", s, 0, t, half)
    for s in both:
        yield ("M", s, 0)
        yield ("f1", s, 0, 0)
    for s in both:
        yield ("den", s)
        for c in range(4):
            yield ("wide_out", s, 0, c)
    for s in both:
        for c in range(2):
            yield ("mlp2", s, c)
    for s in both:
        yield ("rows", s, 1)
    for s in both:
        for t in range(4):
            yield ("h", s, 1, t, 0)
    for s in both:
        yield ("M", s, 1)
        yield ("f1", s, 1, 0)
    for s in both:
        for t in range(4):
            yield ("wide_out", s, 1, t)
    for s in both:
        for q in range(2):
            yield ("res", s, q)
    for l in MULTI:
        for s in both:
            for k in range(2):
                yield ("xT", s, l, k)
        for s in both:
            yield ("rows", s, l)
        for s in both:
            for t in range(4):
                yield ("h", s, l, t, 0)
        for s in both:
            yield ("M", s, l)
            yield ("f1", s, l, 0)
        for h in range(HEADS[l]):
            for s in both:
                if h + 1 < HEADS[l]:
                    yield ("f1", s, l, h + 1)
                yield ("T", s, l, h)
                yield ("N", s, l, h)
        if l == 2:
            for s in both:
                for k in range(2):
                    yield ("oT", s, k)
            for s in both:
                for q in range(2):
                    yield ("wout", s, q)


def build_program(nc, x_in, adj, mlp1_w, mlp1_b, mlp2_w, mlp2_b, W_fc, a_fc, W_hand, a_hand,
                  L1_W, L1_a_src, L1_a_dst, L1_beta, L1_W_out, L2_W, L2_a, L3_W, L3_a, y_out):
    B, NODES, D = x_in.shape
    HID = mlp1_w.shape[1]
    NT = NODES // P
    KD = D // P
    KH = HID // P
    ROUNDS = B // STREAMS
    assert NODES == 512 and D == 256 and HID == 512 and B % STREAMS == 0

    order = list(tensor_jobs())
    place, uses = {}, [0] * BANKS
    for n, job in enumerate(order):
        place[job] = (n % BANKS, uses[n % BANKS])
        uses[n % BANKS] += 1
    tenants = [[job for job in order if place[job][0] == b] for b in range(BANKS)]
    before = {job: of_bank[n - 1] for of_bank in tenants for n, job in enumerate(of_bank)}
    first_head = {2: 0, 3: 8, 4: 12}

    with ExitStack() as ctx:
        def sb(name, shape, dt=F32):
            return ctx.enter_context(nc.sbuf_tensor(name, shape, dt))

        banks = [ctx.enter_context(nc.psum_tensor(f"bank{b}", [P, 512], F32)) for b in range(BANKS)]
        ready = [Signal(ctx, nc, f"bank{b}_ready", uses[b]) for b in range(BANKS)]

        def bank(job):
            return banks[place[job][0]]

        def is_ready(job, it):
            b, n = place[job]
            return ready[b].sem, ready[b].upto(it, n + 1)

        ident = sb("ident", [P, P])
        ident16 = sb("ident16", [P, P], BF16)
        ones = sb("ones", [P, P])
        sel = sb("sel", [64, 8, P], F32R)
        neg_one = sb("neg_one", [P, 1])
        plus_one = sb("plus_one", [P, 1])
        eps_prior = sb("eps_prior", [P, 1])
        minus_half = sb("minus_half", [P, NT])
        maskT = sb("maskT", [P, NT, NODES], BF16)
        priorT = sb("priorT", [P, NT, NODES], BF16)
        w1 = sb("w1", [P, KD, HID])
        b1 = sb("b1", [P, KH])
        w2 = sb("w2", [P, KH, D])
        b2 = sb("b2", [P, KD])
        woT = sb("woT", [P, KD, D])
        KIN = {0: KH, 1: KD, 2: KD, 3: KD, 4: KD}
        WEXT = {0: HID + 1, 1: D + 1, 2: D + 16, 3: D + 8, 4: D + 8}
        wx = {l: sb(f"wx{l}", [P, KIN[l], WEXT[l]]) for l in HEADS}
        wrow = {l: sb(f"wrow{l}", [P, KIN[l], 64]) for l in HEADS}

        class Stream:
            pass

        S = []
        for s in range(STREAMS):
            st = Stream()
            st.x_in = sb(f"x_in{s}", [P, NT, D])
            st.x = sb(f"x{s}", [P, NT, D])
            st.t = sb(f"t{s}", [P, NT, D])
            st.xT = sb(f"xT{s}", [P, KD, NODES])
            st.region = region = sb(f"region{s}", [P, 3 * 8 * 2 * 33 * NT])
            wide = KH * NODES
            st.oT = region[:, 0:wide].rearrange("p (k n) -> p k n", k=KH)
            st.pT = region[:, wide:2 * wide].rearrange("p (k n) -> p k n", k=NT)
            st.h0 = region[:, 2 * wide:2 * wide + NT * (HID + 1)].rearrange("p (k n) -> p k n", k=NT)
            st.parts = {}
            for l in MULTI:
                H, F = HEADS[l], D // HEADS[l]
                n = NT * H * 2 * (F + 1)
                st.parts[l] = [region[:, k * n:(k + 1) * n].rearrange(
                    "p (t h a f) -> p t h a f", t=NT, h=H, a=2) for k in range(3)]
            st.h1 = sb(f"h1_{s}", [P, NT, D + 2])
            st.hf = sb(f"hf{s}", [P, NT, D + 16])
            st.o3T = sb(f"o3T{s}", [P, KD, NODES])
            st.rb = sb(f"rb{s}", [P, NODES])
            st.zb = st.rden = sb(f"zb{s}", [P, NODES])
            st.hp = sb(f"hp{s}", [P, NT, D])
            st.eb = sb(f"eb{s}", [P, NT, D])
            st.tm = sb(f"tm{s}", [P, NT, NODES], BF16)
            st.nm = sb(f"nm{s}", [P, NT, NODES], BF16)
            st.fr = sb(f"fr{s}", [64, NODES], F32R)
            st.mx = sb(f"mx{s}", [8, 1])
            st.dg = sb(f"dg{s}", [8, 8])
            st.M = sb(f"M{s}", [P, 8])
            st.u2 = sb(f"u2_{s}", [P, NT, 8])
            st.z = sb(f"z{s}", [P, NT, 8])
            st.nf2 = sb(f"nf2_{s}", [P, NT, 8])
            st.u = sb(f"u{s}", [P, NT])
            st.v = sb(f"v{s}", [P, NT])
            st.r = sb(f"r{s}", [P, NT, 8])
            st.q = sb(f"q{s}", [P, NT, 65])
            st.num = sb(f"num{s}", [P, NT, 65])
            st.rec = sb(f"rec{s}", [P, NT])
            st.bn = sb(f"bn{s}", [P, NT, 6])
            st.mv = sb(f"mv{s}", [P, NT, 2])
            st.ve = sb(f"ve{s}", [P, NT])
            st.rstd = sb(f"rstd{s}", [P, NT])

            def signal(name, per, s=s):
                return Signal(ctx, nc, f"{name}{s}", per)

            st.x_loaded = signal("x_loaded", 16)
            st.x_in_used = signal("x_in_used", 2)
            st.y_stored = signal("y_stored", 16)
            st.xT_ready = signal("xT_ready", 10)
            st.mlp1_ready = signal("mlp1_ready", 4)
            st.mlp2_ready = signal("mlp2_ready", 2)
            st.h_ready = signal("h_ready", 24)
            st.exp_ready = signal("exp_ready", 15)
            st.elu1 = signal("elu1_", 10)
            st.elu2 = signal("elu2_", 6)
            st.row_steps = signal("row_steps", 20)
            st.col_steps = signal("col_steps", 21)
            st.pT_steps = signal("pT_steps", 12)
            st.rden_ready = signal("rden_ready", 1)
            st.y_steps = signal("y_steps", 12)
            st.low_ready = signal("low_ready", 10)
            st.sum1 = signal("sum1_", 10)
            st.sum2 = signal("sum2_", 6)
            st.t_ready = signal("t_ready", 6)
            st.T_ready = signal("T_ready", 64)
            st.N_ready = signal("N_ready", 16)
            st.head_steps = signal("head_steps", 64)
            st.product_ready = signal("product_ready", 24)
            st.rest1_ready = signal("rest1_ready", 12)
            st.norm_steps = signal("norm_steps", 4 * 14)
            st.rest2_ready = signal("rest2_ready", 12)
            st.rstd_ready = signal("rstd_ready", 4)
            S.append(st)

        XT0 = {0: 0, 2: 2, "oT": 4, 3: 6, 4: 8}
        H0 = {0: 0, 1: 8, 2: 12, 3: 16, 4: 20}
        COL0 = {0: 0, 1: 3, 2: 6, 3: 11, 4: 16}
        PT0 = {0: 0, 1: 4}
        LOW0 = {0: 0, 1: 4, 3: 6, 4: 8}
        NORM0 = {1: 0, 2: 14, 3: 28, 4: 42}
        T0 = {2: 0, 3: 2, 4: 4}
        X0 = {2: 0, 3: 8, 4: 16}
        R0 = {2: 0, 3: 4, 4: 8}


        def emptied(job):
            name, s, *at = job
            st = S[s]
            l = at[0] if at else None
            if name == "xT":
                return st.xT_ready, XT0[l] + at[1] + 1
            if name == "oT":
                return st.xT_ready, XT0["oT"] + at[0] + 1
            if name == "mlp1":
                return st.mlp1_ready, at[0] + 1
            if name == "mlp2":
                return st.mlp2_ready, at[0] + 1
            if name == "rows":
                return st.row_steps, 4 * l + 3
            if name == "h":
                return st.h_ready, H0[l] + (2 * at[1] + at[2] if l == 0 else at[1]) + 1
            if name == "M":
                return st.col_steps, COL0[l] + 1
            if name == "f1":
                return (st.col_steps, COL0[l] + 3) if l in WIDE else (st.T_ready, 4 * (first_head[l] + at[1] + 1))
            if name == "den":
                return st.rden_ready, 1
            if name == "wide_out":
                return st.y_steps, at[1] + 1 if l == 0 else KH + 2 * at[1] + 2
            if name == "res":
                return st.sum2, KH + at[0] + 1
            if name == "N":
                return st.head_steps, 4 * (first_head[l] + at[1]) + 1
            if name == "T":
                return st.head_steps, 4 * (first_head[l] + at[1]) + 2
            assert name == "wout"
            return st.t_ready, T0[2] + at[0] + 1

        def half(x, q):
            return x[:, 2 * q:2 * q + 2, :].rearrange("p t d -> p (t d)")

        def flat(x, t):
            return x[:, t].rearrange("p h a f -> p (h a f)")

        def upper(x, t):
            return flat(x, t).bitcast(BF16)[:, 1::2]

        n_adj = NT * NODES
        adj_int = S[0].region[:, 0:n_adj].bitcast(I32)
        logs = S[0].region[:, n_adj:2 * n_adj]
        maskf = S[0].region[:, 2 * n_adj:3 * n_adj]
        logs_t = logs.rearrange("p (t n) -> p t n", t=NT)
        mask16, prior16 = S[0].tm, S[0].nm
        wo_nat = S[1].hp
        sel_f = S[0].eb[0:64, :, :].rearrange("p t d -> p (t d)").rearrange("p (h n) -> p h n", h=8)
        bt = S[1].M
        rowmax = S[1].rec
        att_vec, off = {}, 0
        for l in HEADS:
            n = HID if l == 0 else D
            for part in range(2):
                att_vec[l, part] = S[1].region[:, off:off + n]
                off += n
        prod = S[1].region[:, off:off + KH * HID]

        loads = ctx.enter_context(nc.semaphore("setup_loads"))
        const_made = ctx.enter_context(nc.semaphore("const_made"))
        setup_v = ctx.enter_context(nc.semaphore("setup_vector"))
        setup_a = ctx.enter_context(nc.semaphore("setup_scalar"))
        setup_t = ctx.enter_context(nc.semaphore("setup_tensor"))
        N_LOADS = 4 + 2 * KD + 1 + 6 + 2 + 8 + 5
        N_CONST = 10 + 2 * STREAMS
        V_TRANSPOSED = {}

        block = ctx.enter_context(nc.Block())

        @block.sync
        def _(sp):
            n_loads = [0]

            def load(dst, src, **kw):
                sp.dma_start(dst, src, **kw).then_inc(loads, 16)
                n_loads[0] += 1

            load(adj_int.rearrange("p (t n) -> p t n", t=NT), adj.rearrange("(t p) n -> p t n", p=P))
            load(bt[:, 0:1], L1_beta.partition_broadcast(P))
            load(wx[0][:, :, 0:HID], W_fc.rearrange("(k p) n -> p k n", p=P))
            load(wx[1][:, :, 0:D], W_hand.rearrange("(k p) n -> p k n", p=P))
            for l, w in ((2, L1_W), (3, L2_W)):
                for k in range(KD):
                    load(wx[l][:, k, 0:D].rearrange("p (h f) -> p h f", h=HEADS[l]),
                         w[:, k * P:(k + 1) * P, :].rearrange("h p f -> p h f"))
            load(wx[4][:, :, 0:D], L3_W.rearrange("(k p) n -> p k n", p=P))
            for part in range(2):
                F = D // 4
                load(att_vec[0, part], a_fc[part * HID:(part + 1) * HID, 0].partition_broadcast(P))
                load(att_vec[1, part], a_hand[part * D:(part + 1) * D, 0].partition_broadcast(P))
                load(att_vec[2, part], (L1_a_src, L1_a_dst)[part].rearrange("h f -> (h f)").partition_broadcast(P))
                load(att_vec[3, part].rearrange("p (h f) -> p h f", h=4),
                     L2_a[:, part * F:(part + 1) * F].partition_broadcast(P))
                for h in range(4):
                    load(att_vec[4, part][:, h * F:(h + 1) * F],
                         L3_a[part * F:(part + 1) * F].partition_broadcast(P))
            load(w1[:, :, :], mlp1_w.rearrange("(k p) n -> p k n", p=P))
            load(w2[:, :, :], mlp2_w.rearrange("(k p) n -> p k n", p=P))
            load(wo_nat[:, 0:KD, :], L1_W_out.rearrange("(k p) n -> p k n", p=P))
            load(b1[:, :], mlp1_b.rearrange("(k p) -> p k", p=P), allow_slow_non_contiguous=True)
            load(b2[:, :], mlp2_b.rearrange("(k p) -> p k", p=P), allow_slow_non_contiguous=True)
            assert n_loads[0] == N_LOADS

            def load_x(it):
                for s, st in enumerate(S):
                    sp.dma_start(st.x_in[:, :, :], x_in[bass.ds(it * STREAMS + s, 1), :, :].rearrange(
                        "o (t p) d -> p (o t) d", p=P)).then_inc(st.x_loaded.sem, 16)

            def store_y(it):
                for s, st in enumerate(S):
                    sp.wait_ge(st.norm_steps.sem, st.norm_steps.upto(it, NORM0[4] + 14))
                    sp.dma_start(y_out[bass.ds(it * STREAMS + s, 1), :, :].rearrange(
                        "o (t p) d -> p (o t) d", p=P), st.t[:, :, :]).then_inc(st.y_stored.sem, 16)

            load_x(0)
            with sp.Fori(0, ROUNDS - 1) as it:
                for st in S:
                    sp.wait_ge(st.x_in_used.sem, st.x_in_used.upto(it, 2))
                load_x(it + 1)
                store_y(it)
            store_y(ROUNDS - 1)
            for st in S:
                sp.wait_ge(st.y_stored.sem, 16 * ROUNDS)

        @block.gpsimd
        def _(gp):
            gp.memset(ident[:, :], 0.0).then_inc(const_made, 1)
            gp.memset(sel_f[:, :, :], 0.0).then_inc(const_made, 1)
            gp.wait_ge(const_made, 2)
            gp.affine_select(out=ident[:, :], in_=ident[:, :], compare_op=ALU.not_equal, fill=1.0, base=0,
                             pattern=[[-1, P]], channel_multiplier=1).then_inc(const_made, 1)
            gp.affine_select(out=sel_f[:, :, :], in_=sel_f[:, :, :], compare_op=ALU.not_equal, fill=1.0,
                             base=0, pattern=[[-1, 8], [0, P]], channel_multiplier=1).then_inc(const_made, 1)
            gp.wait_ge(const_made, 4)
            gp.affine_select(out=sel_f[:, :, :], in_=sel_f[:, :, :], compare_op=ALU.not_equal, fill=1.0,
                             base=-32, pattern=[[-1, 8], [0, P]], channel_multiplier=1).then_inc(const_made, 1)
            gp.memset(ones[:, :], 1.0).then_inc(const_made, 1)
            gp.memset(neg_one[:, :], -1.0).then_inc(const_made, 1)
            gp.memset(plus_one[:, :], 1.0).then_inc(const_made, 1)
            gp.memset(eps_prior[:, :], EPS_PRIOR).then_inc(const_made, 1)
            gp.memset(minus_half[:, :], -0.5).then_inc(const_made, 1)
            for st in S:
                gp.memset(st.fr[:, :].bitcast(F32), 0.0).then_inc(const_made, 1)
                gp.memset(st.h1[:, :, D + 1:D + 2], 1.0).then_inc(const_made, 1)
            gp.wait_ge(setup_v, V_SETUP)

            with gp.Fori(0, ROUNDS) as it:
                def rstd(l):
                    for st in S:
                        gp.wait_ge(st.norm_steps.sem, st.norm_steps.upto(it, NORM0[l] + 10))
                        gp.tensor_tensor(st.rstd[:, :], st.ve[:, :], minus_half[:, :], ALU.pow).then_inc(
                            st.rstd_ready.sem, 1)

                rstd(1)
                for l in MULTI:
                    for st in S:
                        x0, x1, x2 = st.parts[l]
                        for t in range(NT):
                            gp.wait_ge(st.rest1_ready.sem, st.rest1_ready.upto(it, R0[l] + t + 1))
                            gp.tensor_tensor(flat(x2, t), flat(x1, t), upper(x1, t), ALU.subtract).then_inc(
                                st.rest2_ready.sem, 1)
                    rstd(l)

        @block.vector
        def _(dve):
            done = [0]

            def step(ins, wait=True):
                ins.then_inc(setup_v, 1)
                done[0] += 1
                if wait:
                    dve.wait_ge(setup_v, done[0])

            dve.wait_ge(loads, 16 * N_LOADS)
            step(dve.tensor_scalar(bt[:, 1:2], bt[:, 0:1], -1.0, None, ALU.mult))
            step(dve.tensor_tensor(bt[:, 1:2], bt[:, 0:1], bt[:, 1:2], ALU.max))
            step(dve.tensor_scalar(bt[:, 6:7], bt[:, 0:1], 0.0, None, ALU.max), False)
            step(dve.tensor_scalar(logs, adj_int, 0.0, None, ALU.max), False)
            step(dve.tensor_scalar(maskf, adj_int, 0.0, None, ALU.is_gt))
            dve.wait_ge(setup_a, 3)
            step(dve.tensor_reduce(rowmax[:, :], logs_t, AX.X, ALU.max))
            for t in range(NT):
                step(dve.tensor_scalar(logs_t[:, t, :], logs_t[:, t, :], rowmax[:, t:t + 1], None, ALU.subtract))
            step(dve.tensor_tensor(bt[:, 5:6], bt[:, 6:7], bt[:, 3:4], ALU.add))
            assert done[0] == 11
            dve.wait_ge(const_made, N_CONST)
            step(dve.tensor_copy(mask16[:, :, :].rearrange("p t n -> p (t n)"), maskf))
            dve.wait_ge(setup_a, 4)
            step(dve.tensor_tensor(prior16[:, :, :].rearrange("p t n -> p (t n)"), logs, maskf, ALU.mult))
            step(dve.tensor_copy(ident16[:, :], ident[:, :]))
            V_TRANSPOSED["masks"] = done[0]
            step(dve.tensor_copy(sel[:, :, :], sel_f[:, :, :]))
            for l in HEADS:
                H, K, N = HEADS[l], KIN[l], (HID if l == 0 else D)
                step(dve.memset(wrow[l][:, :, :], 0.0))
                for part in range(2):
                    pr = prod[:, 0:K * N].rearrange("p (k n) -> p k n", k=K)
                    step(dve.tensor_tensor(pr, wx[l][:, :, 0:N],
                                           att_vec[l, part].unsqueeze(1).broadcast_to([P, K, N]), ALU.mult))
                    to = wrow[l][:, :, 32 * part:32 * part + H]
                    step(dve.tensor_reduce(to, prod[:, 0:K * N].rearrange("p (k h f) -> p k h f", k=K, h=H),
                                           AX.X, ALU.add))
                    if l in MULTI or part == 1:
                        col = N if l in WIDE else D + part * H
                        step(dve.tensor_copy(wx[l][:, :, col:col + H], to))
            for n in range(2 * NT):
                dve.wait_ge(setup_t, n + 1)
                step(dve.tensor_copy((maskT, priorT)[n // NT][:, n % NT, :],
                                     banks[n][:, :].bitcast(BF16)[:, 0:NODES]), False)
            V_TRANSPOSED["banks"] = done[0]
            for k in range(KD):
                dve.wait_ge(setup_t, 2 * NT + k + 1)
                step(dve.tensor_copy(woT[:, k, :], banks[k][:, 0:D]), False)
            dve.wait_ge(setup_v, done[0])
            assert done[0] == V_SETUP, done[0]

            with dve.Fori(0, ROUNDS) as it:
                def score_rows(l):
                    H = HEADS[l]
                    for s, st in enumerate(S):
                        done, n = st.row_steps, 4 * l
                        rows = bank(("rows", s, l))
                        dve.wait_ge(*is_ready(("rows", s, l), it))
                        dve.tensor_reduce(st.mx[0:H, :], rows[32:32 + H, :], AX.X, ALU.max).then_inc(done.sem, 1)
                        dve.tensor_copy(st.fr[0:H, :], rows[0:H, :]).then_inc(done.sem, 1)
                        dve.wait_ge(done.sem, done.upto(it, n + 2))
                        dve.tensor_tensor(st.fr[32:32 + H, :], rows[0:H, :], st.fr[0:H, :].bitcast(F32),
                                          ALU.subtract).then_inc(done.sem, 1)
                        dve.tensor_scalar(st.dg[0:H, 0:H], ident[0:H, 0:H], st.mx[0:H, 0:1], None,
                                          ALU.mult).then_inc(done.sem, 1)

                def score_columns(l):
                    H = HEADS[l]
                    for s, st in enumerate(S):
                        done, n = st.col_steps, COL0[l]
                        dve.wait_ge(*is_ready(("M", s, l), it))
                        dve.tensor_copy(st.M[:, 0:H], bank(("M", s, l))[:, 0:H]).then_inc(done.sem, 1)
                        dve.wait_ge(st.h_ready.sem, st.h_ready.upto(it, H0[l] + (8 if l == 0 else 4)))
                        dve.wait_ge(done.sem, done.upto(it, n + 1))
                        M = st.M[:, 0:H].unsqueeze(1).broadcast_to([P, NT, H])
                        if l in WIDE:
                            f2 = st.h0[:, :, HID:HID + 1] if l == 0 else st.h1[:, :, D:D + 1]
                            dve.tensor_tensor(st.u2[:, :, 0:1], f2, M, ALU.subtract).then_inc(done.sem, 1)
                            dve.wait_ge(*is_ready(("f1", s, l, 0), it))
                            dve.tensor_scalar(st.zb[:, :], bank(("f1", s, l, 0))[:, :], st.M[:, 0:1], Z_MIN,
                                              ALU.add, ALU.max).then_inc(done.sem, 1)
                            continue
                        f1, f2 = st.hf[:, :, D:D + H], st.hf[:, :, D + H:D + 2 * H]
                        dve.tensor_tensor(st.u2[:, :, 0:H], f2, M, ALU.subtract).then_inc(done.sem, 1)
                        dve.tensor_tensor(st.z[:, :, 0:H], f1, M, ALU.add).then_inc(done.sem, 1)
                        dve.wait_ge(done.sem, done.upto(it, n + 3))
                        dve.tensor_scalar(st.z[:, :, 0:H], st.z[:, :, 0:H], Z_MIN, None, ALU.max).then_inc(done.sem, 1)
                        dve.tensor_scalar(st.nf2[:, :, 0:H], f2, -1.0, None, ALU.mult).then_inc(done.sem, 1)

                def wide_weights(l):
                    for st in S:
                        dve.wait_ge(st.exp_ready.sem, st.exp_ready.upto(it, 3 * l + 3))
                        for t in range(NT):
                            dve.tensor_scalar(st.pT[:, t, :], st.rb[:, :], st.v[:, t:t + 1], st.u[:, t:t + 1],
                                              ALU.mult, ALU.max).then_inc(st.pT_steps.sem, 1)
                        if l == 1:
                            for t in range(NT):
                                dve.wait_ge(st.pT_steps.sem, st.pT_steps.upto(it, NT + t + 1))
                                dve.tensor_tensor(st.pT[:, t, :], st.pT[:, t, :], maskT[:, t, :],
                                                  ALU.mult).then_inc(st.pT_steps.sem, 1)

                def low(st, k, out, y):
                    dve.tensor_scalar(out, y, 0.0, None, ALU.min).then_inc(st.low_ready.sem, 1)

                def norm(l):
                    for st in S:
                        if l == 1:
                            dve.wait_ge(st.x_in_used.sem, st.x_in_used.upto(it, 2))
                        else:
                            dve.wait_ge(st.t_ready.sem, st.t_ready.upto(it, T0[l] + 2))
                        for t in range(NT):
                            dve.bn_stats(st.bn[:, t, :], st.t[:, t, :]).then_inc(st.norm_steps.sem, 1)
                    for st in S:
                        dve.wait_ge(st.norm_steps.sem, st.norm_steps.upto(it, NORM0[l] + NT))
                        dve.memset(st.ve[:, :], EPS_LN).then_inc(st.norm_steps.sem, 1)
                        for t in range(NT):
                            dve.bn_aggr(st.mv[:, t, :], st.bn[:, t, :]).then_inc(st.norm_steps.sem, 1)
                    for st in S:
                        dve.wait_ge(st.norm_steps.sem, st.norm_steps.upto(it, NORM0[l] + 9))
                        dve.tensor_tensor(st.ve[:, :], st.mv[:, :, 1], st.ve[:, :], ALU.add).then_inc(
                            st.norm_steps.sem, 1)
                    for st in S:
                        dve.wait_ge(st.rstd_ready.sem, st.rstd_ready.upto(it, l))
                        out = st.t if l == 4 else st.x
                        for t in range(NT):
                            dve.tensor_scalar(out[:, t, :], st.t[:, t, :], st.mv[:, t, 0:1], st.rstd[:, t:t + 1],
                                              ALU.subtract, ALU.mult).then_inc(st.norm_steps.sem, 1)

                def rest1(st, l, t):
                    x0, x1, _ = st.parts[l]
                    dve.wait_ge(st.product_ready.sem, st.product_ready.upto(it, X0[l] + 2 * t + 2))
                    dve.tensor_tensor(flat(x1, t), flat(x0, t), upper(x0, t), ALU.subtract).then_inc(
                        st.rest1_ready.sem, 1)

                score_rows(0)
                score_columns(0)
                wide_weights(0)
                for s, st in enumerate(S):
                    dve.wait_ge(*is_ready(("den", s), it))
                    dve.reciprocal(st.rden[:, :], bank(("den", s))[:, :]).then_inc(st.rden_ready.sem, 1)
                    dve.wait_ge(st.rden_ready.sem, st.rden_ready.upto(it, 1))
                    for c in range(KH + 1):
                        if c < KH:
                            y, e = half(st.hp, c % 2), half(st.eb, c % 2)
                            dve.wait_ge(*is_ready(("wide_out", s, 0, c), it))
                            if c >= 2:
                                dve.wait_ge(st.sum2.sem, st.sum2.upto(it, c - 1))
                            dve.tensor_tensor(y, bank(("wide_out", s, 0, c))[:, :], st.rden[:, :],
                                              ALU.mult).then_inc(st.y_steps.sem, 1)
                            dve.wait_ge(st.y_steps.sem, st.y_steps.upto(it, c + 1))
                            low(st, c, e, y)
                        if c >= 1:
                            c1 = c - 1
                            y, e, o = half(st.hp, c1 % 2), half(st.eb, c1 % 2), st.oT[:, c1, :]
                            dve.wait_ge(st.elu2.sem, st.elu2.upto(it, c1 + 1))
                            dve.scalar_tensor_tensor(out=e, in0=e, scalar=-1.0, in1=o, op0=ALU.add,
                                                     op1=ALU.add).then_inc(st.sum1.sem, 1)
                            dve.wait_ge(st.sum1.sem, st.sum1.upto(it, c1 + 1))
                            dve.scalar_tensor_tensor(out=o, in0=y, scalar=0.0, in1=e, op0=ALU.max,
                                                     op1=ALU.add).then_inc(st.sum2.sem, 1)

                score_rows(1)
                score_columns(1)
                wide_weights(1)
                for s, st in enumerate(S):
                    for q in range(2):
                        for t in (2 * q, 2 * q + 1):
                            out = bank(("wide_out", s, 1, t))
                            dve.wait_ge(*is_ready(("wide_out", s, 1, t), it))
                            dve.reciprocal(st.rec[:, t:t + 1], out[:, D + 1:D + 2]).then_inc(st.y_steps.sem, 1)
                            dve.wait_ge(st.y_steps.sem, st.y_steps.upto(it, KH + 2 * t + 1))
                            dve.tensor_scalar(st.hp[:, t, :], out[:, 0:D], st.rec[:, t:t + 1], None,
                                              ALU.mult).then_inc(st.y_steps.sem, 1)
                        dve.wait_ge(st.y_steps.sem, st.y_steps.upto(it, KH + 4 * q + 4))
                        low(st, q, half(st.eb, q), half(st.hp, q))
                for s, st in enumerate(S):
                    for q in range(2):
                        y, e = half(st.hp, q), half(st.eb, q)
                        dve.wait_ge(st.elu2.sem, st.elu2.upto(it, KH + q + 1))
                        dve.scalar_tensor_tensor(out=y, in0=y, scalar=0.0, in1=e, op0=ALU.max,
                                                 op1=ALU.add).then_inc(st.sum1.sem, 1)
                        dve.wait_ge(st.sum1.sem, st.sum1.upto(it, KH + q + 1))
                        dve.wait_ge(*is_ready(("res", s, q), it))
                        dve.scalar_tensor_tensor(out=y, in0=y, scalar=-1.0, in1=bank(("res", s, q))[:, :],
                                                 op0=ALU.add, op1=ALU.add).then_inc(st.sum2.sem, 1)
                        dve.wait_ge(st.sum2.sem, st.sum2.upto(it, KH + q + 1))
                        if q == 0:
                            dve.wait_ge(st.x_loaded.sem, st.x_loaded.upto(it, 16))
                            dve.wait_ge(st.y_stored.sem, st.y_stored.upto(it, 0))
                        dve.scalar_tensor_tensor(out=half(st.t, q), in0=y, scalar=0.0, in1=half(st.x_in, q),
                                                 op0=ALU.max, op1=ALU.add).then_inc(st.x_in_used.sem, 1)
                norm(1)

                for l in MULTI:
                    H = HEADS[l]
                    F = D // H
                    score_rows(l)
                    score_columns(l)
                    for st in S:
                        x0, x1, _ = st.parts[l]
                        dve.wait_ge(st.exp_ready.sem, st.exp_ready.upto(it, 3 * l + 2))
                        for t in range(NT):
                            h = st.hf[:, t, 0:D].rearrange("p (h f) -> p h f", h=H)
                            for a in range(2):
                                dve.tensor_tensor(x0[:, t, :, a, 0:F], h,
                                                  x0[:, t, :, a, F:F + 1].broadcast_to([P, H, F]),
                                                  ALU.mult).then_inc(st.product_ready.sem, 1)
                            if t:
                                rest1(st, l, t - 1)
                        rest1(st, l, NT - 1)

                    def weights(s, h):
                        st, g = S[s], first_head[l] + h
                        mask = priorT if l == 2 else maskT
                        dve.wait_ge(*is_ready(("f1", s, l, h), it))
                        if h:
                            dve.wait_ge(*is_ready(("T", s, l, h - 1), it))
                        for t in range(NT):
                            dve.scalar_tensor_tensor(out=st.tm[:, t, :], in0=bank(("f1", s, l, h))[:, :],
                                                     scalar=st.nf2[:, t, h:h + 1], in1=mask[:, t, :],
                                                     op0=ALU.is_gt, op1=ALU.mult).then_inc(st.T_ready.sem, 1)
                        if h:
                            dve.wait_ge(*is_ready(("N", s, l, h - 1), it))
                        dve.wait_ge(st.T_ready.sem, st.T_ready.upto(it, 4 * g + 4))
                        dve.tensor_tensor(st.nm[:, :, :].rearrange("p t n -> p (t n)"),
                                          mask[:, :, :].rearrange("p t n -> p (t n)"),
                                          st.tm[:, :, :].rearrange("p t n -> p (t n)"),
                                          ALU.subtract).then_inc(st.N_ready.sem, 1)

                    def combine(s, h):
                        st, done, n = S[s], S[s].head_steps, 4 * (first_head[l] + h)
                        tb = bank(("T", s, l, h))[:, 0:NT * (F + 1)].rearrange("p (t f) -> p t f", t=NT)
                        nb = bank(("N", s, l, h))[:, 0:NT * (F + 1)].rearrange("p (t f) -> p t f", t=NT)
                        q, num = st.q[:, :, 0:F + 1], st.num[:, :, 0:F + 1]
                        dve.wait_ge(*is_ready(("N", s, l, h), it))
                        if h == 0:
                            dve.wait_ge(st.exp_ready.sem, st.exp_ready.upto(it, 3 * l + 3))
                        dve.tensor_tensor(q, nb, st.r[:, :, h:h + 1].broadcast_to([P, NT, F + 1]),
                                          ALU.mult).then_inc(done.sem, 1)
                        dve.wait_ge(done.sem, done.upto(it, n + 1))
                        dve.tensor_tensor(num, tb, q, ALU.add).then_inc(done.sem, 1)
                        dve.wait_ge(done.sem, done.upto(it, n + 2))
                        dve.reciprocal(st.rec[:, :], st.num[:, :, F]).then_inc(done.sem, 1)
                        dve.wait_ge(done.sem, done.upto(it, n + 3))
                        dve.tensor_tensor(st.hp[:, :, h * F:(h + 1) * F], st.num[:, :, 0:F],
                                          st.rec[:, :].unsqueeze(2).broadcast_to([P, NT, F]),
                                          ALU.mult).then_inc(done.sem, 1)

                    steps = [(s, h) for h in range(H) for s in range(STREAMS)]
                    for n, (s, h) in enumerate(steps):
                        weights(s, h)
                        if n:
                            combine(*steps[n - 1])
                    combine(*steps[-1])

                    last = 4 * (first_head[l] + H)
                    if l == 2:
                        for s, st in enumerate(S):
                            for q in range(2):
                                dve.wait_ge(*is_ready(("wout", s, q), it))
                                dve.tensor_tensor(half(st.t, q), bank(("wout", s, q))[:, :], half(st.x, q),
                                                  ALU.add).then_inc(st.t_ready.sem, 1)
                    else:
                        for st in S:
                            dve.wait_ge(st.head_steps.sem, st.head_steps.upto(it, last))
                            for q in range(2):
                                low(st, q, half(st.eb, q), half(st.hp, q))
                        for st in S:
                            for q in range(2):
                                y, e, n = half(st.hp, q), half(st.eb, q), LOW0[l] + q + 1
                                dve.wait_ge(st.elu1.sem, st.elu1.upto(it, n))
                                dve.scalar_tensor_tensor(out=y, in0=y, scalar=0.0, in1=e, op0=ALU.max,
                                                         op1=ALU.add).then_inc(st.sum1.sem, 1)
                                dve.wait_ge(st.sum1.sem, st.sum1.upto(it, n))
                                dve.scalar_tensor_tensor(out=half(st.t, q), in0=y, scalar=-1.0, in1=half(st.x, q),
                                                         op0=ALU.add, op1=ALU.add).then_inc(st.t_ready.sem, 1)
                    norm(l)

        @block.scalar
        def _(act):
            act.wait_ge(const_made, N_CONST)
            act.wait_ge(setup_v, 3)
            act.activation(bt[:, 2:3], bt[:, 1:2], ACT.Exp, scale=-1.0).then_inc(setup_a, 1)
            act.wait_ge(setup_a, 1)
            act.activation(bt[:, 3:4], bt[:, 2:3], ACT.Ln, bias=plus_one[:, 0:1]).then_inc(setup_a, 1)
            act.wait_ge(setup_v, 4)
            act.activation(logs, logs, ACT.Ln, bias=eps_prior[:, 0:1]).then_inc(setup_a, 1)
            act.wait_ge(setup_v, 11)
            act.activation(logs, logs, ACT.Exp, scale=bt[:, 5:6]).then_inc(setup_a, 1)
            act.wait_ge(setup_v, V_SETUP)

            with act.Fori(0, ROUNDS) as it:
                def copy(job, out, signal, n=NODES):
                    act.wait_ge(*is_ready(job, it))
                    act.activation(out, bank(job)[:, 0:n], ACT.Copy).then_inc(signal.sem, 1)

                def relu(job, out, signal, bias):
                    act.wait_ge(*is_ready(job, it))
                    act.activation(out, bank(job)[:, :], ACT.Relu, bias=bias).then_inc(signal.sem, 1)

                def transposed(l):
                    for s, st in enumerate(S):
                        for k in range(KD):
                            copy(("oT", s, k) if l == "oT" else ("xT", s, l, k), st.xT[:, k, :], st.xT_ready)

                def exps(l):
                    H = HEADS[l]
                    F = D // H
                    for st in S:
                        act.wait_ge(st.col_steps.sem, st.col_steps.upto(it, COL0[l] + 2))
                        arg = st.u2[:, :, 0:H]
                        if l in WIDE:
                            u, v = st.u[:, :].unsqueeze(2), st.v[:, :].unsqueeze(2)
                        else:
                            u, v = (st.parts[l][0][:, :, :, a, F] for a in range(2))
                        act.activation(u, arg, ACT.Exp).then_inc(st.exp_ready.sem, 1)
                        act.activation(v, arg, ACT.Exp, scale=SLOPE).then_inc(st.exp_ready.sem, 1)
                        act.wait_ge(st.col_steps.sem, st.col_steps.upto(it, COL0[l] + (3 if l in WIDE else 4)))
                        z, r = (st.zb[:, :], st.rb[:, :]) if l in WIDE else (st.z[:, :, 0:H], st.r[:, :, 0:H])
                        act.activation(r, z, ACT.Exp, scale=SLOPE - 1.0).then_inc(st.exp_ready.sem, 1)

                def elu_exps(st, l, k, piece, twice):
                    act.wait_ge(st.low_ready.sem, st.low_ready.upto(it, LOW0[l] + k + 1))
                    act.activation(piece, piece, ACT.Exp).then_inc(st.elu1.sem, 1)
                    if twice:
                        act.wait_ge(st.elu1.sem, st.elu1.upto(it, LOW0[l] + k + 1))
                        act.activation(piece, piece, ACT.Exp, bias=neg_one[:, 0:1]).then_inc(st.elu2.sem, 1)

                transposed(0)
                for s, st in enumerate(S):
                    for c in range(KH):
                        relu(("mlp1", s, c), st.oT[:, c, :], st.mlp1_ready, b1[:, c:c + 1])
                for s, st in enumerate(S):
                    for t in range(NT):
                        copy(("h", s, 0, t, 0), st.h0[:, t, 0:D], st.h_ready, D)
                        copy(("h", s, 0, t, 1), st.h0[:, t, D:HID + 1], st.h_ready, HID + 1 - D)
                exps(0)
                for st in S:
                    for c in range(KH):
                        elu_exps(st, 0, c, half(st.eb, c % 2), True)
                for s, st in enumerate(S):
                    for c in range(KD):
                        relu(("mlp2", s, c), st.o3T[:, c, :], st.mlp2_ready, b2[:, c:c + 1])
                for s, st in enumerate(S):
                    for t in range(NT):
                        copy(("h", s, 1, t, 0), st.h1[:, t, 0:D + 1], st.h_ready, D + 1)
                exps(1)
                for st in S:
                    for q in range(2):
                        elu_exps(st, 1, q, half(st.eb, q), True)
                for l in MULTI:
                    n = D + 2 * HEADS[l]
                    transposed(l)
                    for s, st in enumerate(S):
                        for t in range(NT):
                            copy(("h", s, l, t, 0), st.hf[:, t, 0:n], st.h_ready, n)
                    exps(l)
                    if l == 2:
                        transposed("oT")
                    else:
                        for st in S:
                            for q in range(2):
                                elu_exps(st, l, q, half(st.eb, q), False)

        @block.tensor
        def _(pe):
            pe.wait_ge(setup_v, V_TRANSPOSED["masks"])
            for n in range(2 * NT):
                src, j = (mask16, prior16)[n // NT], n % NT
                for t in range(NT):
                    last = pe.transpose(banks[n][:, :].bitcast(BF16)[:, t * P:(t + 1) * P],
                                        src[:, t, j * P:(j + 1) * P], ident16[:, :])
                last.then_inc(setup_t, 1)
            pe.wait_ge(setup_v, V_TRANSPOSED["banks"])
            for k in range(KD):
                for o in range(KD):
                    last = pe.transpose(banks[k][:, o * P:(o + 1) * P], wo_nat[:, o, k * P:(k + 1) * P], ident[:, :])
                last.then_inc(setup_t, 1)
            pe.wait_ge(setup_v, V_SETUP)

            with pe.Fori(0, ROUNDS) as it:
                ahead = list(order)

                def begin(job):
                    assert ahead.pop(0) == job
                    prev = before[job]
                    signal, n = emptied(prev)
                    if order.index(prev) < order.index(job):
                        pe.wait_ge(signal.sem, signal.upto(it, n))
                    else:
                        pe.wait_ge(signal.sem, signal.upto(it, 0))
                    return bank(job)

                def end(job, last):
                    last.then_inc(ready[place[job][0]].sem, 1)

                def transposes(job, src, pieces):
                    out = begin(job)
                    for n, (t, k) in enumerate(pieces):
                        last = pe.transpose(out[:, n * P:(n + 1) * P], src[:, t, k * P:(k + 1) * P], ident[:, :])
                    end(job, last)

                def products(job, K, lhsT, rhs, n, m=P):
                    out = begin(job)
                    for k in range(K):
                        last = pe.matmul(out[0:m, 0:n], lhsT(k), rhs(k), start=(k == 0), stop=(k == K - 1))
                    end(job, last)

                def rows_of(l, inT):
                    for s, st in enumerate(S):
                        products(("rows", s, l), KIN[l], lambda k: wrow[l][:, k, :], lambda k: inT(st)[:, k, :],
                                 NODES, 64)

                def f1_row(s, l, h):
                    st = S[s]
                    job = ("f1", s, l, h)
                    out = begin(job)
                    if h == 0:
                        pe.wait_ge(st.row_steps.sem, st.row_steps.upto(it, 4 * l + 4))
                    end(job, pe.matmul(out[:, :], sel[:, h, :], st.fr[:, :], start=True, stop=True))

                def maxima_and_f1(l):
                    H = HEADS[l]
                    for s, st in enumerate(S):
                        job = ("M", s, l)
                        out = begin(job)
                        pe.wait_ge(st.row_steps.sem, st.row_steps.upto(it, 4 * l + 4))
                        end(job, pe.matmul(out[:, 0:H], ones[0:H, :], st.dg[0:H, 0:H], start=True, stop=True))
                        f1_row(s, l, 0)

                def node_tile(x, t):
                    return lambda k: x[:, k, t * P:(t + 1) * P]

                for s, st in enumerate(S):
                    pe.wait_ge(st.x_loaded.sem, st.x_loaded.upto(it, 16))
                    for k in range(KD):
                        transposes(("xT", s, 0, k), st.x_in, [(t, k) for t in range(NT)])
                for s, st in enumerate(S):
                    pe.wait_ge(st.xT_ready.sem, st.xT_ready.upto(it, XT0[0] + KD))
                    for c in range(KH):
                        products(("mlp1", s, c), KD, lambda k: w1[:, k, c * P:(c + 1) * P],
                                 lambda k: st.xT[:, k, :], NODES)
                for st in S:
                    pe.wait_ge(st.mlp1_ready.sem, st.mlp1_ready.upto(it, KH))
                rows_of(0, lambda st: st.oT)
                for s, st in enumerate(S):
                    for t in range(NT):
                        products(("h", s, 0, t, 0), KH, node_tile(st.oT, t), lambda k: wx[0][:, k, 0:D], D)
                        products(("h", s, 0, t, 1), KH, node_tile(st.oT, t), lambda k: wx[0][:, k, D:HID + 1],
                                 HID + 1 - D)
                maxima_and_f1(0)
                for s, st in enumerate(S):
                    pe.wait_ge(st.pT_steps.sem, st.pT_steps.upto(it, NT))
                    products(("den", s), NT, lambda k: ones[:, :], lambda k: st.pT[:, k, :], NODES)
                    for c in range(KH):
                        products(("wide_out", s, 0, c), NT, lambda k: st.h0[:, k, c * P:(c + 1) * P],
                                 lambda k: st.pT[:, k, :], NODES)
                for s, st in enumerate(S):
                    pe.wait_ge(st.sum2.sem, st.sum2.upto(it, KH))
                    for c in range(KD):
                        products(("mlp2", s, c), KH, lambda k: w2[:, k, c * P:(c + 1) * P],
                                 lambda k: st.oT[:, k, :], NODES)
                for st in S:
                    pe.wait_ge(st.mlp2_ready.sem, st.mlp2_ready.upto(it, KD))
                rows_of(1, lambda st: st.o3T)
                for s, st in enumerate(S):
                    for t in range(NT):
                        products(("h", s, 1, t, 0), KD, node_tile(st.o3T, t), lambda k: wx[1][:, k, :], D + 1)
                maxima_and_f1(1)
                for s, st in enumerate(S):
                    pe.wait_ge(st.pT_steps.sem, st.pT_steps.upto(it, 3 * NT))
                    for t in range(NT):
                        products(("wide_out", s, 1, t), NT, node_tile(st.pT, t), lambda k: st.h1[:, k, :], D + 2)
                for s, st in enumerate(S):
                    for q in range(2):
                        transposes(("res", s, q), st.o3T,
                                   [(k, t) for t in (2 * q, 2 * q + 1) for k in range(KD)])

                for l in MULTI:
                    H = HEADS[l]
                    F = D // H
                    for s, st in enumerate(S):
                        pe.wait_ge(st.norm_steps.sem, st.norm_steps.upto(it, NORM0[l - 1] + 14))
                        for k in range(KD):
                            transposes(("xT", s, l, k), st.x, [(t, k) for t in range(NT)])
                    for st in S:
                        pe.wait_ge(st.xT_ready.sem, st.xT_ready.upto(it, XT0[l] + KD))
                    rows_of(l, lambda st: st.xT)
                    for s, st in enumerate(S):
                        for t in range(NT):
                            products(("h", s, l, t, 0), KD, node_tile(st.xT, t), lambda k: wx[l][:, k, :], D + 2 * H)
                    maxima_and_f1(l)
                    for h in range(H):
                        for s, st in enumerate(S):
                            g = first_head[l] + h
                            if h + 1 < H:
                                f1_row(s, l, h + 1)
                            if h == 0:
                                pe.wait_ge(st.rest2_ready.sem, st.rest2_ready.upto(it, R0[l] + NT))
                            for name, w, a in (("T", st.tm, 0), ("N", st.nm, 1)):
                                out = begin((name, s, l, h))
                                if name == "T":
                                    pe.wait_ge(st.T_ready.sem, st.T_ready.upto(it, 4 * g + 4))
                                else:
                                    pe.wait_ge(st.N_ready.sem, st.N_ready.upto(it, g + 1))
                                for t in range(NT):
                                    for j in range(NT):
                                        for part in range(3):
                                            x = st.parts[l][part][:, j, h, a, :].bitcast(BF16)[:, 1::2]
                                            last = pe.matmul(out[:, t * (F + 1):(t + 1) * (F + 1)],
                                                             w[:, j, t * P:(t + 1) * P], x,
                                                             start=(j == 0 and part == 0),
                                                             stop=(j == NT - 1 and part == 2))
                                end((name, s, l, h), last)
                    if l == 2:
                        for s, st in enumerate(S):
                            pe.wait_ge(st.head_steps.sem, st.head_steps.upto(it, 4 * H))
                            for k in range(KD):
                                transposes(("oT", s, k), st.hp, [(t, k) for t in range(NT)])
                        for s, st in enumerate(S):
                            pe.wait_ge(st.xT_ready.sem, st.xT_ready.upto(it, XT0["oT"] + KD))
                            for q in range(2):
                                out = begin(("wout", s, q))
                                for n in range(2):
                                    t = 2 * q + n
                                    for k in range(KD):
                                        last = pe.matmul(out[:, n * D:(n + 1) * D], st.xT[:, k, t * P:(t + 1) * P],
                                                         woT[:, k, :], start=(k == 0), stop=(k == KD - 1))
                                end(("wout", s, q), last)
                assert not ahead


_INS = ["x", "adj", "L0_gnn_mlp1_w", "L0_gnn_mlp1_b", "L0_gnn_mlp2_w", "L0_gnn_mlp2_b", "L0_gnn_W_fc",
        "L0_gnn_a_fc", "L0_gnn_W_hand", "L0_gnn_a_hand", "L1_gnn_W", "L1_gnn_a_src", "L1_gnn_a_dst",
        "L1_gnn_beta_tilde", "L1_gnn_W_out", "L2_gnn_W", "L2_gnn_a", "L3_gnn_W", "L3_gnn_a"]


def kernel(**inputs):
    import concourse.bacc as bacc
    import numpy as np
    from concourse.bass_utils import run_bass_kernel_spmd

    nc = bacc.Bacc("TRN2", target_bir_lowering=False, num_devices=1)
    arrays, args = {}, []
    for name in _INS:
        a = np.ascontiguousarray(inputs[name])
        if a.ndim == 0:
            a = a.reshape(1)
        arrays[f"in_{name}_dram"] = a
        args.append(nc.dram_tensor(f"in_{name}_dram", a.shape, mybir.dt.from_np(a.dtype), kind="ExternalInput").ap())
    out = nc.dram_tensor("out_0_dram", inputs["x"].shape, mybir.dt.float32, kind="ExternalOutput").ap()
    build_program(nc, *args, out)
    r = run_bass_kernel_spmd(nc, [arrays], core_ids=[0])
    return r.results[0]["out_0_dram"]
```

```python
from contextlib import ExitStack

import concourse.bass as bass
from concourse import mybir

ALU = mybir.AluOpType
ACT = mybir.ActivationFunctionType
AX = mybir.AxisListType
F32 = mybir.dt.float32
F32R = mybir.dt.float32r
BF16 = mybir.dt.bfloat16
I32 = mybir.dt.int32

P = 128
STREAMS = 2
BANKS = 8
EPS_LN = 1e-5
EPS_PRIOR = 1e-6
SLOPE = 0.2
Z_MIN = -75.0
STEEP = 2.0 ** 100
STEPS_A_REGISTER = 8
V_SETUP = 45

HEADS = {0: 1, 1: 1, 2: 8, 3: 4, 4: 4}
WIDE = (0, 1)
MULTI = (2, 3, 4)
FIRST_HEAD = {2: 0, 3: 8, 4: 12}
TM_RING, NM_RING = 3, 2


SCHEDULE = {
    "tensor": """
        ~h.2.0 ~h.2.1 ~h.2.2 ~h.2.3 xT.0 mlp1.0 ~rows.2 mlp1.1 mlp1.2 ~score.2 ~f1.2.1 mlp1.3 h.0.0 ~f1.2.2
        ~f1.2.3 ~all_v.0 ~heads.2.0 ~all_v.1 ~all_v.2 ~all_v.3 ~heads.2.1 ~f1.2.4 ~heads.2.2 ~f1.2.5 ~f1.2.6
        h.0.1 ~heads.2.3 ~heads.2.4 ~f1.2.7 h.0.2 ~heads.2.5 ~heads.2.6 h.0.3 ~heads.2.7 rows.0 ~oT score.0
        ~wout.0 ~wout.1 den ~xT.3 ~h.3.0 ~h.3.1 ~h.3.2 ~h.3.3 ~rows.3 wide_out.0.0 ~score.3 ~f1.3.1 wide_out.0.1
        wide_out.0.2 ~f1.3.2 ~heads.3.0 ~f1.3.3 wide_out.0.3 ~heads.3.1 ~heads.3.2 ~heads.3.3 mlp2.0 mlp2.1
        h.1.0 h.1.1 h.1.2 h.1.3 rows.1 ~xT.4 score.1 ~h.4.0 ~h.4.1 ~h.4.2 ~h.4.3 ~rows.4 wide_out.1.0
        wide_out.1.1 ~score.4 ~f1.4.1 res.1 ~f1.4.2 wide_out.1.2 wide_out.1.3 ~f1.4.3 res.0 ~heads.4.0
        ~heads.4.1 ~heads.4.2 xT.2 ~heads.4.3""",
    "vector": """
        ~rows.2 ~score.2 ~products.2.0 ~products.2.1 ~products.2.2 ~products.2.3 ~products.2.4 ~T.2.0 ~T.2.1
        ~T.2.2 ~combine.2.0.0 ~combine.2.0.1 ~combine.2.0.2 ~combine.2.0.3 ~combine.2.0.4 ~combine.2.1.0
        ~combine.2.1.1 ~combine.2.1.2 ~combine.2.1.3 ~combine.2.1.4 ~combine.2.2.0 ~combine.2.2.1 ~combine.2.2.2
        ~T.2.3 ~T.2.4 ~combine.2.2.3 ~combine.2.2.4 ~T.2.5 ~T.2.6 ~combine.2.3.0 ~combine.2.3.1 ~combine.2.3.2
        ~combine.2.3.3 ~combine.2.3.4 ~T.2.7 ~combine.2.4.0 ~combine.2.4.1 ~combine.2.4.2 ~combine.2.4.3
        ~combine.2.4.4 ~combine.2.5.0 ~combine.2.5.1 ~combine.2.5.2 ~combine.2.5.3 ~combine.2.5.4 ~combine.2.6.0
        ~combine.2.6.1 ~combine.2.6.2 ~combine.2.6.3 ~combine.2.6.4 ~combine.2.7.0 ~combine.2.7.1 ~combine.2.7.2
        ~combine.2.7.3 ~combine.2.7.4 rows.0 score.0 wide_weights.0 ~residual2.0 ~residual2.1 ~stats.2 ~norm.2
        den ~rows.3 ~score.3 ~products.3.0 ~products.3.1 ~products.3.2 ~products.3.3 ~products.3.4 ~T.3.0 ~T.3.1
        divide.0 ~N.3.0 divide.1 fold.0 ~N.3.1 ~combine.3.0.0 divide.2 ~combine.3.0.1 ~T.3.2 ~T.3.3 ~N.3.2
        fold.1 ~combine.3.0.2 ~N.3.3 ~combine.3.0.3 divide.3 ~combine.3.1.0 fold.2 ~combine.3.1.1 fold.3
        ~combine.3.1.2 ~combine.3.1.3 ~combine.3.2.0 ~combine.3.2.1 ~combine.3.2.2 ~combine.3.2.3 ~combine.3.3.0
        ~combine.3.3.1 ~combine.3.3.2 ~combine.3.3.3 ~low.3.0 ~low.3.1 ~residual3.3.0 ~residual3.3.1 ~stats.3
        ~norm.3 rows.1 score.1 wide_weights.1 ~rows.4 divide1.0 ~score.4 divide1.1 ~products.4.0 ~products.4.1
        ~products.4.2 ~products.4.3 ~products.4.4 ~T.4.0 ~T.4.1 ~N.4.0 divide1.2 divide1.3 ~N.4.1 ~T.4.2
        residual1.0 ~combine.4.0.0 residual1.1 stats.1 ~combine.4.0.1 ~N.4.2 norm.1 ~combine.4.0.2 ~T.4.3
        ~combine.4.0.3 ~combine.4.1.0 ~N.4.3 ~combine.4.1.1 ~combine.4.1.2 ~combine.4.1.3 ~combine.4.2.0
        ~combine.4.2.1 ~combine.4.2.2 ~combine.4.2.3 ~combine.4.3.0 ~combine.4.3.1 ~combine.4.3.2 ~combine.4.3.3
        ~low.4.0 ~low.4.1 ~residual3.4.0 ~residual3.4.1 ~stats.4 ~norm.4""",
    "scalar": """
        ~h.2.0 ~h.2.1 ~h.2.2 xT.0 ~h.2.3 mlp1.0 ~exps.2 mlp1.1 mlp1.2 mlp1.3 ~step.2.0 ~step.2.1 ~all_v.0
        ~step.2.2 h.0.0 ~step.2.3 ~all_v.1 ~all_v.2 ~all_v.3 ~step.2.4 ~step.2.5 h.0.1 ~step.2.6 ~step.2.7 h.0.2
        h.0.3 ~oT exps.0 ~xT.3 ~h.3.0 ~h.3.1 ~h.3.2 ~h.3.3 ~exps.3 ~step.3.0 ~step.3.1 ~step.3.2 elu.0.0 elu.0.1
        ~step.3.3 elu.0.2 elu.0.3 mlp2.0 ~elu.3.0 mlp2.1 ~elu.3.1 h.1.0 h.1.1 h.1.2 h.1.3 ~xT.4 exps.1 ~h.4.0
        ~h.4.1 ~h.4.2 ~h.4.3 ~exps.4 elu.1.0 ~step.4.0 ~step.4.1 ~step.4.2 elu.1.1 ~step.4.3 xT.2 ~elu.4.0
        ~elu.4.1""",
    "gpsimd": """
        ~rest2.2.0 ~rest2.2.1 ~rest2.2.2 ~rest2.2.3 ~rstd.2 ~rest2.3.0 ~rest2.3.1 ~rest2.3.2 ~rest2.3.3 ~rstd.3
        ~rest2.4.0 ~rest2.4.1 ~rest2.4.2 ~rest2.4.3 rstd.1 ~rstd.4""",
}


def timeline():
    steps = []
    for first in range(STREAMS):
        for engine, line in SCHEDULE.items():
            for word in line.split():
                step, *at = word.lstrip("~").split(".")
                s, behind = (1 - first, 1 - first) if word[0] == "~" else (first, 0)
                steps.append((s, behind, engine, step, tuple(int(x) for x in at)))
    return steps


def jobs_of(step, s, *at):
    if step == "xT":
        return [("xT", s, at[0], k) for k in range(2)]
    if step == "oT":
        return [("oT", s, 2, k) for k in range(2)]
    if step == "h":
        return [("h", s, *at, half) for half in range(2 if at[0] == 0 else 1)]
    if step == "rows":
        return [("f1_rows", s, at[0]), ("f2_rows", s, at[0])]
    if step == "score":
        return [("M", s, at[0]), ("f1", s, at[0], 0)]
    if step == "heads":
        return [("T", s, *at)] + [("N", s, *at)] * (at[0] != 2)
    return [(step, s, *at)]


class Ahead:

    def __init__(self, value, by):
        self.value, self.by = value, by


class Signal:

    def __init__(self, ctx, nc, name, per):
        self.sem = ctx.enter_context(nc.semaphore(name))
        self.per = per

    def upto(self, r, k):
        it, behind = r if isinstance(r, tuple) else (r, 0)
        if isinstance(it, Ahead):
            it, behind = it.value, behind + it.by
        return it * self.per + (k - behind * self.per)


def build_program(nc, x_in, adj, mlp1_w, mlp1_b, mlp2_w, mlp2_b, W_fc, a_fc, W_hand, a_hand,
                  L1_W, L1_a_src, L1_a_dst, L1_beta, L1_W_out, L2_W, L2_a, L3_W, L3_a, y_out):
    B, NODES, D = x_in.shape
    HID = mlp1_w.shape[1]
    NT = NODES // P
    KD = D // P
    KH = HID // P
    ROUNDS = B // STREAMS
    assert NODES == 512 and D == 256 and HID == 512 and B % STREAMS == 0 and ROUNDS >= 3
    KIN = {0: KH, 1: KD, 2: KD, 3: KD, 4: KD}
    WIDTH = {0: HID, 1: D, 2: D, 3: D, 4: D}

    steps = timeline()

    body_jobs = [(job, behind) for s, behind, engine, step, at in steps if engine == "tensor"
                 for job in jobs_of(step, s, *at)]
    behind_of = dict(body_jobs)
    bank_of = {job: n % BANKS for n, (job, _) in enumerate(body_jobs)}
    number = {}
    for s in range(STREAMS):
        mine = [job for lag in (0, 1) for job, behind in body_jobs if job[1] == s and behind == lag]
        number.update({job: n for n, job in enumerate(mine)})
    jobs_per_round = len(number) // STREAMS

    def chain(users):
        return {job: (users[:n][::-1], users[-1]) for n, job in enumerate(users)}

    bank_before, tm_before, nm_before = {}, {}, {}
    for b in range(BANKS):
        bank_before.update(chain([job for job, _ in body_jobs if bank_of[job] == b]))
    for k in range(TM_RING):
        tm_before.update(chain([job for job, _ in body_jobs
                                if job[0] == "T" and (FIRST_HEAD[job[2]] + job[3]) % TM_RING == k]))
    for k in range(NM_RING):
        nm_before.update(chain([job for job, _ in body_jobs if job[0] == "N" and job[3] % NM_RING == k]))

    def tenant_before(before, it):
        same, last = before
        for job in same:
            if not isinstance(it, int) or behind_of[job] == (it == ROUNDS):
                return job, (it, behind_of[job])
        if isinstance(it, int) and it == 0:
            return None
        assert behind_of[last] == 0, "the first iteration doesn't have it"
        return last, (it, 1)

    with ExitStack() as ctx:
        def sb(name, shape, dt=F32):
            return ctx.enter_context(nc.sbuf_tensor(name, shape, dt))

        banks = [ctx.enter_context(nc.psum_tensor(f"bank{b}", [P, 512], F32)) for b in range(BANKS)]

        def bank(job):
            return banks[bank_of[job]]

        ident = sb("ident", [P, P])
        ident16 = sb("ident16", [P, P], BF16)
        ones = sb("ones", [P, P])
        sel = sb("sel", [64, 8, P], F32R)
        neg_one = sb("neg_one", [P, 1])
        plus_one = sb("plus_one", [P, 1])
        eps_prior = sb("eps_prior", [P, 1])
        minus_half = sb("minus_half", [P, NT])
        maskT = sb("maskT", [P, NT, NODES], BF16)
        priorT = sb("priorT", [P, NT, NODES], BF16)
        w1 = sb("w1", [P, KD, HID])
        b1 = sb("b1", [P, KH])
        w2 = sb("w2", [P, KH, D])
        b2 = sb("b2", [P, KD])
        woT = sb("woT", [P, KD, D])
        wx = {l: sb(f"wx{l}", [P, KIN[l], WIDTH[l] + 2 * HEADS[l]]) for l in HEADS}
        tm = [sb(f"tm{k}", [P, NT, NODES], BF16) for k in range(TM_RING)]
        nm = [sb(f"nm{k}", [P, NT, NODES], BF16) for k in range(NM_RING)]

        class Stream:
            pass

        S = []
        for s in range(STREAMS):
            st = Stream()
            st.x_in = sb(f"x_in{s}", [P, NT, D])
            st.x = sb(f"x{s}", [P, NT, D])
            st.t = sb(f"t{s}", [P, NT, D])
            st.xT = sb(f"xT{s}", [P, KD, NODES])
            st.region = region = sb(f"region{s}", [P, 3 * 8 * 2 * 33 * NT])
            wide = KH * NODES
            st.oT = region[:, 0:wide].rearrange("p (k n) -> p k n", k=KH)
            st.pT = region[:, wide:2 * wide].rearrange("p (k n) -> p k n", k=NT)
            st.h0 = region[:, 2 * wide:2 * wide + NT * (HID + 2)].rearrange("p (k n) -> p k n", k=NT)
            st.parts = {}
            for l in MULTI:
                H, F = HEADS[l], D // HEADS[l]
                n = NT * H * 2 * (F + 1)
                st.parts[l] = [region[:, k * n:(k + 1) * n].rearrange(
                    "p (t h a f) -> p t h a f", t=NT, h=H, a=2) for k in range(3)]
            st.h1 = sb(f"h1_{s}", [P, NT, D + 3])
            st.hf = sb(f"hf{s}", [P, NT, D + 16])
            st.o3T = sb(f"o3T{s}", [P, KD, NODES])
            st.zb = st.rb = st.rden = sb(f"zb{s}", [P, NODES])
            st.hp = sb(f"hp{s}", [P, NT, D])
            st.eb = sb(f"eb{s}", [P, NT, D])
            st.vh = sb(f"vh{s}", [P, NT, 8 * 33])
            st.fr = sb(f"fr{s}", [64, NODES], F32R)
            st.mx = sb(f"mx{s}", [8, 1])
            st.dg = sb(f"dg{s}", [8, 8])
            st.M = sb(f"M{s}", [P, 8])
            st.u2 = sb(f"u2_{s}", [P, NT, 8])
            st.z = sb(f"z{s}", [P, NT, 8])
            st.steep = sb(f"steep{s}", [P, NT, 8])
            st.u = sb(f"u{s}", [P, NT])
            st.v = sb(f"v{s}", [P, NT])
            st.r = sb(f"r{s}", [P, NT, 8])
            st.q = sb(f"q{s}", [P, NT, 65])
            st.num = sb(f"num{s}", [P, NT, 65])
            st.rec = sb(f"rec{s}", [P, NT])
            st.bn = sb(f"bn{s}", [P, NT, 6])
            st.mv = sb(f"mv{s}", [P, NT, 2])
            st.ve = sb(f"ve{s}", [P, NT])
            st.rstd = sb(f"rstd{s}", [P, NT])

            def signal(name, per, s=s):
                return Signal(ctx, nc, f"{name}{s}", per)

            st.x_loaded = signal("x_loaded", 16)
            st.x_in_used = signal("x_in_used", 2)
            st.y_stored = signal("y_stored", 16)
            st.product_done = signal("product_done", jobs_per_round)
            st.xT_ready = signal("xT_ready", 10)
            st.mlp1_ready = signal("mlp1_ready", 4)
            st.mlp2_ready = signal("mlp2_ready", 2)
            st.h_ready = signal("h_ready", 24)
            st.exp_ready = signal("exp_ready", 15)
            st.elu1 = signal("elu1_", 10)
            st.elu2 = signal("elu2_", 6)
            st.step_ready = signal("step_ready", 64)
            st.vh_ready = signal("vh_ready", 4)
            st.row_steps = signal("row_steps", 20)
            st.col_steps = signal("col_steps", 21)
            st.pT_steps = signal("pT_steps", 12)
            st.rden_ready = signal("rden_ready", 1)
            st.y_steps = signal("y_steps", 12)
            st.low_ready = signal("low_ready", 12)
            st.sum1 = signal("sum1_", 10)
            st.sum2 = signal("sum2_", 6)
            st.t_ready = signal("t_ready", 6)
            st.T_ready = signal("T_ready", 16)
            st.N_ready = signal("N_ready", 8)
            st.head_steps = signal("head_steps", 8 * 5 + 8 * 4)
            st.product_ready = signal("product_ready", 24)
            st.rest1_ready = signal("rest1_ready", 12)
            st.norm_steps = signal("norm_steps", 4 * 14)
            st.rest2_ready = signal("rest2_ready", 12)
            st.rstd_ready = signal("rstd_ready", 4)
            S.append(st)

        XT0 = {0: 0, 2: 2, "oT": 4, 3: 6, 4: 8}
        H0 = {0: 0, 1: 8, 2: 12, 3: 16, 4: 20}
        COL0 = {0: 0, 1: 3, 2: 6, 3: 11, 4: 16}
        LOW0 = {0: 0, 1: 4, 3: 8, 4: 10}
        ELU0 = {0: 0, 1: 4, 3: 6, 4: 8}
        NORM0 = {1: 0, 2: 14, 3: 28, 4: 42}
        T0 = {2: 0, 3: 2, 4: 4}
        X0 = {2: 0, 3: 8, 4: 16}
        R0 = {2: 0, 3: 4, 4: 8}

        def head_step(l, h, k):
            return 5 * h + k if l == 2 else 40 + 4 * (FIRST_HEAD[l] - 8 + h) + k

        def is_ready(job, r):
            done = S[job[1]].product_done
            return done.sem, done.upto(r, number[job] + 1)

        def emptied(job):
            name, s, *at = job
            st = S[s]
            l = at[0] if at else None
            if name == "xT":
                return st.xT_ready, XT0[l] + at[1] + 1
            if name == "oT":
                return st.xT_ready, XT0["oT"] + at[1] + 1
            if name == "mlp1":
                return st.mlp1_ready, at[0] + 1
            if name == "mlp2":
                return st.mlp2_ready, at[0] + 1
            if name == "f2_rows":
                return st.row_steps, 4 * l + 1
            if name == "f1_rows":
                return st.row_steps, 4 * l + 3
            if name == "h":
                return st.h_ready, H0[l] + (2 * at[1] + at[2] if l == 0 else at[1]) + 1
            if name == "M":
                return st.col_steps, COL0[l] + 1
            if name == "f1":
                return (st.col_steps, COL0[l] + 3) if l in WIDE else (st.step_ready, 4 * (FIRST_HEAD[l] + at[1] + 1))
            if name == "den":
                return st.rden_ready, 1
            if name == "wide_out":
                return st.low_ready, LOW0[l] + at[1] + 1
            if name == "res":
                return st.sum2, KH + at[0] + 1
            if name == "all_v":
                return st.vh_ready, at[0] + 1
            if name == "N":
                return st.head_steps, head_step(*at, 1)
            if name == "T":
                return st.head_steps, head_step(*at, 3 if l == 2 else 2)
            assert name == "wout"
            return st.t_ready, T0[2] + at[0] + 1

        def half(x, q):
            return x[:, 2 * q:2 * q + 2, :].rearrange("p t d -> p (t d)")

        def flat(x, t):
            return x[:, t].rearrange("p h a f -> p (h a f)")

        def upper(x, t):
            return flat(x, t).bitcast(BF16)[:, 1::2]

        def score_columns(l, st):
            x = {0: st.h0, 1: st.h1}.get(l, st.hf)
            N, H = WIDTH[l], HEADS[l]
            return x[:, :, N:N + H], x[:, :, N + H:N + 2 * H]

        def whole_iteration(engine, name, steps_of):
            mine = [(s, behind, step, at) for s, behind, e, step, at in steps if e == name]

            def run(it, lags):
                now = it
                for n, (s, behind, step, at) in enumerate(mine):
                    if n % STEPS_A_REGISTER == 0 and not isinstance(it, int):
                        by = n // STEPS_A_REGISTER + 1
                        now = Ahead(engine.snap(it + by), by)
                    if behind in lags:
                        steps_of(now)[step](S[s], s, (now, behind), *at)

            run(0, (0,))
            with engine.Fori(1, ROUNDS) as it:
                run(it, (0, 1))
            run(ROUNDS, (1,))

        n_adj = NT * NODES
        adj_int = S[0].region[:, 0:n_adj].bitcast(I32)
        logs = S[0].region[:, n_adj:2 * n_adj]
        maskf = S[0].region[:, 2 * n_adj:3 * n_adj]
        logs_t = logs.rearrange("p (t n) -> p t n", t=NT)
        mask16, prior16 = tm[0], nm[0]
        wo_nat = S[1].hp
        sel_f = S[0].eb[0:64, :, :].rearrange("p t d -> p (t d)").rearrange("p (h n) -> p h n", h=8)
        bt = S[1].M
        rowmax = S[1].rec
        att_vec, off = {}, 0
        for l in HEADS:
            for part in range(2):
                att_vec[l, part] = S[1].region[:, off:off + WIDTH[l]]
                off += WIDTH[l]
        prod = S[1].region[:, off:off + KH * HID]

        loads = ctx.enter_context(nc.semaphore("setup_loads"))
        const_made = ctx.enter_context(nc.semaphore("const_made"))
        setup_v = ctx.enter_context(nc.semaphore("setup_vector"))
        setup_a = ctx.enter_context(nc.semaphore("setup_scalar"))
        setup_t = ctx.enter_context(nc.semaphore("setup_tensor"))
        N_LOADS = 4 + 2 * KD + 1 + 6 + 2 + 8 + 5
        N_CONST = 10 + 2 * STREAMS
        V_TRANSPOSED = {}

        block = ctx.enter_context(nc.Block())

        @block.sync
        def _(sp):
            n_loads = [0]

            def load(dst, src, **kw):
                sp.dma_start(dst, src, **kw).then_inc(loads, 16)
                n_loads[0] += 1

            load(adj_int.rearrange("p (t n) -> p t n", t=NT), adj.rearrange("(t p) n -> p t n", p=P))
            load(bt[:, 0:1], L1_beta.partition_broadcast(P))
            load(wx[0][:, :, 0:HID], W_fc.rearrange("(k p) n -> p k n", p=P))
            load(wx[1][:, :, 0:D], W_hand.rearrange("(k p) n -> p k n", p=P))
            for l, w in ((2, L1_W), (3, L2_W)):
                for k in range(KD):
                    load(wx[l][:, k, 0:D].rearrange("p (h f) -> p h f", h=HEADS[l]),
                         w[:, k * P:(k + 1) * P, :].rearrange("h p f -> p h f"))
            load(wx[4][:, :, 0:D], L3_W.rearrange("(k p) n -> p k n", p=P))
            for part in range(2):
                F = D // 4
                load(att_vec[0, part], a_fc[part * HID:(part + 1) * HID, 0].partition_broadcast(P))
                load(att_vec[1, part], a_hand[part * D:(part + 1) * D, 0].partition_broadcast(P))
                load(att_vec[2, part], (L1_a_src, L1_a_dst)[part].rearrange("h f -> (h f)").partition_broadcast(P))
                load(att_vec[3, part].rearrange("p (h f) -> p h f", h=4),
                     L2_a[:, part * F:(part + 1) * F].partition_broadcast(P))
                for h in range(4):
                    load(att_vec[4, part][:, h * F:(h + 1) * F],
                         L3_a[part * F:(part + 1) * F].partition_broadcast(P))
            load(w1[:, :, :], mlp1_w.rearrange("(k p) n -> p k n", p=P))
            load(w2[:, :, :], mlp2_w.rearrange("(k p) n -> p k n", p=P))
            load(wo_nat[:, 0:KD, :], L1_W_out.rearrange("(k p) n -> p k n", p=P))
            load(b1[:, :], mlp1_b.rearrange("(k p) -> p k", p=P), allow_slow_non_contiguous=True)
            load(b2[:, :], mlp2_b.rearrange("(k p) -> p k", p=P), allow_slow_non_contiguous=True)
            assert n_loads[0] == N_LOADS

            def load_x(s, r):
                st = S[s]
                sp.dma_start(st.x_in[:, :, :], x_in[bass.ds(r * STREAMS + s, 1), :, :].rearrange(
                    "o (t p) d -> p (o t) d", p=P)).then_inc(st.x_loaded.sem, 16)

            def next_x(s, r):
                sp.wait_ge(S[s].x_in_used.sem, S[s].x_in_used.upto(r, 2))
                load_x(s, r + 1)

            def store_y(s, r):
                st = S[s]
                sp.wait_ge(st.norm_steps.sem, st.norm_steps.upto(r, NORM0[4] + 14))
                sp.dma_start(y_out[bass.ds(r * STREAMS + s, 1), :, :].rearrange(
                    "o (t p) d -> p (o t) d", p=P), st.t[:, :, :]).then_inc(st.y_stored.sem, 16)

            for s in range(STREAMS):
                load_x(s, 0)
            next_x(0, 0)
            store_y(0, 0)
            next_x(1, 0)
            with sp.Fori(1, ROUNDS - 1) as it:
                store_y(1, it - 1)
                next_x(0, it)
                store_y(0, it)
                next_x(1, it)
            store_y(1, ROUNDS - 2)
            store_y(0, ROUNDS - 1)
            store_y(1, ROUNDS - 1)
            for st in S:
                sp.wait_ge(st.y_stored.sem, 16 * ROUNDS)

        @block.gpsimd
        def _(gp):
            gp.memset(ident[:, :], 0.0).then_inc(const_made, 1)
            gp.memset(sel_f[:, :, :], 0.0).then_inc(const_made, 1)
            gp.wait_ge(const_made, 2)
            gp.affine_select(out=ident[:, :], in_=ident[:, :], compare_op=ALU.not_equal, fill=1.0, base=0,
                             pattern=[[-1, P]], channel_multiplier=1).then_inc(const_made, 1)
            gp.affine_select(out=sel_f[:, :, :], in_=sel_f[:, :, :], compare_op=ALU.not_equal, fill=1.0,
                             base=0, pattern=[[-1, 8], [0, P]], channel_multiplier=1).then_inc(const_made, 1)
            gp.wait_ge(const_made, 4)
            gp.affine_select(out=sel_f[:, :, :], in_=sel_f[:, :, :], compare_op=ALU.not_equal, fill=1.0,
                             base=-32, pattern=[[-1, 8], [0, P]], channel_multiplier=1).then_inc(const_made, 1)
            gp.memset(ones[:, :], 1.0).then_inc(const_made, 1)
            gp.memset(neg_one[:, :], -1.0).then_inc(const_made, 1)
            gp.memset(plus_one[:, :], 1.0).then_inc(const_made, 1)
            gp.memset(eps_prior[:, :], EPS_PRIOR).then_inc(const_made, 1)
            gp.memset(minus_half[:, :], -0.5).then_inc(const_made, 1)
            for st in S:
                gp.memset(st.fr[:, :].bitcast(F32), 0.0).then_inc(const_made, 1)
                gp.memset(st.h1[:, :, D + 2:D + 3], 1.0).then_inc(const_made, 1)
            gp.wait_ge(setup_v, V_SETUP)

            def steps_of(it):
                def rstd(st, s, r, l):
                    gp.wait_ge(st.norm_steps.sem, st.norm_steps.upto(r, NORM0[l] + 10))
                    gp.tensor_tensor(st.rstd[:, :], st.ve[:, :], minus_half[:, :], ALU.pow).then_inc(
                        st.rstd_ready.sem, 1)

                def rest2(st, s, r, l, t):
                    x0, x1, x2 = st.parts[l]
                    gp.wait_ge(st.rest1_ready.sem, st.rest1_ready.upto(r, R0[l] + t + 1))
                    gp.tensor_tensor(flat(x2, t), flat(x1, t), upper(x1, t), ALU.subtract).then_inc(
                        st.rest2_ready.sem, 1)

                return {"rstd": rstd, "rest2": rest2}

            whole_iteration(gp, "gpsimd", steps_of)

        @block.vector
        def _(dve):
            done = [0]

            def step(ins, wait=True):
                ins.then_inc(setup_v, 1)
                done[0] += 1
                if wait:
                    dve.wait_ge(setup_v, done[0])

            dve.wait_ge(loads, 16 * N_LOADS)
            step(dve.tensor_scalar(bt[:, 1:2], bt[:, 0:1], -1.0, None, ALU.mult))
            step(dve.tensor_tensor(bt[:, 1:2], bt[:, 0:1], bt[:, 1:2], ALU.max))
            step(dve.tensor_scalar(bt[:, 6:7], bt[:, 0:1], 0.0, None, ALU.max), False)
            step(dve.tensor_scalar(logs, adj_int, 0.0, None, ALU.max), False)
            step(dve.tensor_scalar(maskf, adj_int, 0.0, None, ALU.is_gt))
            dve.wait_ge(setup_a, 3)
            step(dve.tensor_reduce(rowmax[:, :], logs_t, AX.X, ALU.max))
            for t in range(NT):
                step(dve.tensor_scalar(logs_t[:, t, :], logs_t[:, t, :], rowmax[:, t:t + 1], None, ALU.subtract))
            step(dve.tensor_tensor(bt[:, 5:6], bt[:, 6:7], bt[:, 3:4], ALU.add))
            assert done[0] == 11
            dve.wait_ge(const_made, N_CONST)
            step(dve.tensor_copy(mask16[:, :, :].rearrange("p t n -> p (t n)"), maskf))
            dve.wait_ge(setup_a, 4)
            step(dve.tensor_tensor(prior16[:, :, :].rearrange("p t n -> p (t n)"), logs, maskf, ALU.mult))
            step(dve.tensor_copy(ident16[:, :], ident[:, :]))
            V_TRANSPOSED["masks"] = done[0]
            step(dve.tensor_copy(sel[:, :, :], sel_f[:, :, :]))
            for l in HEADS:
                H, K, N = HEADS[l], KIN[l], WIDTH[l]
                for part in range(2):
                    step(dve.tensor_tensor(prod[:, 0:K * N].rearrange("p (k n) -> p k n", k=K), wx[l][:, :, 0:N],
                                           att_vec[l, part].unsqueeze(1).broadcast_to([P, K, N]), ALU.mult))
                    step(dve.tensor_reduce(wx[l][:, :, N + part * H:N + (part + 1) * H],
                                           prod[:, 0:K * N].rearrange("p (k h f) -> p k h f", k=K, h=H),
                                           AX.X, ALU.add))
            for n in range(2 * NT):
                dve.wait_ge(setup_t, n + 1)
                step(dve.tensor_copy((maskT, priorT)[n // NT][:, n % NT, :],
                                     banks[n][:, :].bitcast(BF16)[:, 0:NODES]), False)
            V_TRANSPOSED["banks"] = done[0]
            for k in range(KD):
                dve.wait_ge(setup_t, 2 * NT + k + 1)
                step(dve.tensor_copy(woT[:, k, :], banks[k][:, 0:D]), False)
            dve.wait_ge(setup_v, done[0])
            assert done[0] == V_SETUP, done[0]

            def steps_of(it):
                def rows(st, s, r, l):
                    H, done, n = HEADS[l], st.row_steps, 4 * l
                    f1, f2 = bank(("f1_rows", s, l)), bank(("f2_rows", s, l))
                    dve.wait_ge(*is_ready(("f2_rows", s, l), r))
                    dve.tensor_reduce(st.mx[0:H, :], f2[0:H, :], AX.X, ALU.max).then_inc(done.sem, 1)
                    dve.tensor_copy(st.fr[0:H, :], f1[0:H, :]).then_inc(done.sem, 1)
                    dve.wait_ge(done.sem, done.upto(r, n + 2))
                    dve.tensor_tensor(st.fr[32:32 + H, :], f1[0:H, :], st.fr[0:H, :].bitcast(F32),
                                      ALU.subtract).then_inc(done.sem, 1)
                    dve.tensor_scalar(st.dg[0:H, 0:H], ident[0:H, 0:H], st.mx[0:H, 0:1], None,
                                      ALU.mult).then_inc(done.sem, 1)

                def score(st, s, r, l):
                    H, done, n = HEADS[l], st.col_steps, COL0[l]
                    f1, f2 = score_columns(l, st)
                    dve.wait_ge(*is_ready(("M", s, l), r))
                    dve.tensor_copy(st.M[:, 0:H], bank(("M", s, l))[:, 0:H]).then_inc(done.sem, 1)
                    dve.wait_ge(st.h_ready.sem, st.h_ready.upto(r, H0[l] + (8 if l == 0 else 4)))
                    dve.wait_ge(done.sem, done.upto(r, n + 1))
                    M = st.M[:, 0:H].unsqueeze(1).broadcast_to([P, NT, H])
                    dve.tensor_tensor(st.u2[:, :, 0:H], f2, M, ALU.subtract).then_inc(done.sem, 1)
                    if l in WIDE:
                        dve.wait_ge(*is_ready(("f1", s, l, 0), r))
                        dve.tensor_scalar(st.zb[:, :], bank(("f1", s, l, 0))[:, :], st.M[:, 0:1], Z_MIN,
                                          ALU.add, ALU.max).then_inc(done.sem, 1)
                        return
                    dve.tensor_tensor(st.z[:, :, 0:H], f1, M, ALU.add).then_inc(done.sem, 1)
                    dve.tensor_scalar(st.steep[:, :, 0:H], f2, STEEP, None, ALU.mult).then_inc(done.sem, 1)
                    dve.wait_ge(done.sem, done.upto(r, n + 3))
                    dve.tensor_scalar(st.z[:, :, 0:H], st.z[:, :, 0:H], Z_MIN, None, ALU.max).then_inc(done.sem, 1)

                def wide_weights(st, s, r, l):
                    dve.wait_ge(st.exp_ready.sem, st.exp_ready.upto(r, 3 * l + 3))
                    for t in range(NT):
                        dve.tensor_scalar(st.pT[:, t, :], st.rb[:, :], st.v[:, t:t + 1], st.u[:, t:t + 1],
                                          ALU.mult, ALU.max).then_inc(st.pT_steps.sem, 1)
                    if l == 1:
                        for t in range(NT):
                            dve.wait_ge(st.pT_steps.sem, st.pT_steps.upto(r, NT + t + 1))
                            dve.tensor_tensor(st.pT[:, t, :], st.pT[:, t, :], maskT[:, t, :],
                                              ALU.mult).then_inc(st.pT_steps.sem, 1)

                def den(st, s, r):
                    dve.wait_ge(*is_ready(("den", s), r))
                    dve.reciprocal(st.rden[:, :], bank(("den", s))[:, :]).then_inc(st.rden_ready.sem, 1)

                def divide(st, s, r, c):
                    out = bank(("wide_out", s, 0, c))
                    dve.wait_ge(*is_ready(("wide_out", s, 0, c), r))
                    if c == 0:
                        dve.wait_ge(st.rden_ready.sem, st.rden_ready.upto(r, 1))
                    if c >= 2:
                        dve.wait_ge(st.sum2.sem, st.sum2.upto(r, c - 1))
                    dve.tensor_tensor(half(st.hp, c % 2), out[:, :], st.rden[:, :], ALU.mult).then_inc(
                        st.y_steps.sem, 1)
                    dve.scalar_tensor_tensor(out=half(st.eb, c % 2), in0=out[:, :], scalar=0.0, in1=st.rden[:, :],
                                             op0=ALU.min, op1=ALU.mult).then_inc(st.low_ready.sem, 1)

                def fold(st, s, r, c):
                    y, e, o = half(st.hp, c % 2), half(st.eb, c % 2), st.oT[:, c, :]
                    dve.wait_ge(st.elu2.sem, st.elu2.upto(r, c + 1))
                    dve.scalar_tensor_tensor(out=e, in0=e, scalar=-1.0, in1=o, op0=ALU.add,
                                             op1=ALU.add).then_inc(st.sum1.sem, 1)
                    dve.wait_ge(st.sum1.sem, st.sum1.upto(r, c + 1))
                    dve.scalar_tensor_tensor(out=o, in0=y, scalar=0.0, in1=e, op0=ALU.max,
                                             op1=ALU.add).then_inc(st.sum2.sem, 1)

                def divide1(st, s, r, t):
                    out = bank(("wide_out", s, 1, t))
                    dve.wait_ge(*is_ready(("wide_out", s, 1, t), r))
                    dve.reciprocal(st.rec[:, t:t + 1], out[:, D + 2:D + 3]).then_inc(st.y_steps.sem, 1)
                    dve.wait_ge(st.y_steps.sem, st.y_steps.upto(r, KH + 2 * t + 1))
                    dve.tensor_scalar(st.hp[:, t, :], out[:, 0:D], st.rec[:, t:t + 1], None,
                                      ALU.mult).then_inc(st.y_steps.sem, 1)
                    dve.tensor_scalar(st.eb[:, t, :], out[:, 0:D], st.rec[:, t:t + 1], 0.0,
                                      ALU.mult, ALU.min).then_inc(st.low_ready.sem, 1)

                def residual1(st, s, r, q):
                    y, e = half(st.hp, q), half(st.eb, q)
                    dve.wait_ge(st.elu2.sem, st.elu2.upto(r, KH + q + 1))
                    dve.scalar_tensor_tensor(out=y, in0=y, scalar=0.0, in1=e, op0=ALU.max,
                                             op1=ALU.add).then_inc(st.sum1.sem, 1)
                    dve.wait_ge(st.sum1.sem, st.sum1.upto(r, KH + q + 1))
                    dve.wait_ge(*is_ready(("res", s, q), r))
                    dve.scalar_tensor_tensor(out=y, in0=y, scalar=-1.0, in1=bank(("res", s, q))[:, :],
                                             op0=ALU.add, op1=ALU.add).then_inc(st.sum2.sem, 1)
                    dve.wait_ge(st.sum2.sem, st.sum2.upto(r, KH + q + 1))
                    if q == 0:
                        dve.wait_ge(st.x_loaded.sem, st.x_loaded.upto(r, 16))
                        dve.wait_ge(st.y_stored.sem, st.y_stored.upto(r, 0))
                    dve.scalar_tensor_tensor(out=half(st.t, q), in0=y, scalar=0.0, in1=half(st.x_in, q),
                                             op0=ALU.max, op1=ALU.add).then_inc(st.x_in_used.sem, 1)

                def stats(st, s, r, l):
                    done, n = st.norm_steps, NORM0[l]
                    for t in range(NT):
                        if t % 2 == 0 and l == 1:
                            dve.wait_ge(st.x_in_used.sem, st.x_in_used.upto(r, t // 2 + 1))
                        elif t % 2 == 0:
                            dve.wait_ge(st.t_ready.sem, st.t_ready.upto(r, T0[l] + t // 2 + 1))
                        dve.bn_stats(st.bn[:, t, :], st.t[:, t, :]).then_inc(done.sem, 1)
                    dve.wait_ge(done.sem, done.upto(r, n + NT))
                    dve.memset(st.ve[:, :], EPS_LN).then_inc(done.sem, 1)
                    for t in range(NT):
                        dve.bn_aggr(st.mv[:, t, :], st.bn[:, t, :]).then_inc(done.sem, 1)
                    dve.wait_ge(done.sem, done.upto(r, n + 9))
                    dve.tensor_tensor(st.ve[:, :], st.mv[:, :, 1], st.ve[:, :], ALU.add).then_inc(done.sem, 1)

                def norm(st, s, r, l):
                    dve.wait_ge(st.rstd_ready.sem, st.rstd_ready.upto(r, l))
                    out = st.t if l == 4 else st.x
                    for t in range(NT):
                        dve.tensor_scalar(out[:, t, :], st.t[:, t, :], st.mv[:, t, 0:1], st.rstd[:, t:t + 1],
                                          ALU.subtract, ALU.mult).then_inc(st.norm_steps.sem, 1)

                def products(st, s, r, l, t):
                    H = HEADS[l]
                    F = D // H
                    x0, x1, _ = st.parts[l]
                    if t < NT:
                        h = st.hf[:, t, 0:D].rearrange("p (h f) -> p h f", h=H)
                        if t == 0:
                            dve.wait_ge(st.exp_ready.sem, st.exp_ready.upto(r, 3 * l + 2))
                        for a in range(2):
                            dve.tensor_tensor(x0[:, t, :, a, 0:F], h,
                                              x0[:, t, :, a, F:F + 1].broadcast_to([P, H, F]),
                                              ALU.mult).then_inc(st.product_ready.sem, 1)
                    if t > 0:
                        dve.wait_ge(st.product_ready.sem, st.product_ready.upto(r, X0[l] + 2 * t))
                        dve.tensor_tensor(flat(x1, t - 1), flat(x0, t - 1), upper(x0, t - 1),
                                          ALU.subtract).then_inc(st.rest1_ready.sem, 1)

                def T(st, s, r, l, h):
                    g = FIRST_HEAD[l] + h
                    x = tm[g % TM_RING][:, :, :].rearrange("p t n -> p (t n)")
                    mask = (priorT if l == 2 else maskT)[:, :, :].rearrange("p t n -> p (t n)")
                    dve.wait_ge(st.step_ready.sem, st.step_ready.upto(r, 4 * g + 4))
                    dve.tensor_tensor(x, x, mask, ALU.min).then_inc(st.T_ready.sem, 1)

                def N(st, s, r, l, h):
                    g = FIRST_HEAD[l] + h
                    before = tenant_before(nm_before["N", s, l, h], it)
                    if before:
                        dve.wait_ge(*is_ready(*before))
                    dve.wait_ge(st.T_ready.sem, st.T_ready.upto(r, g + 1))
                    dve.tensor_tensor(nm[h % NM_RING][:, :, :].rearrange("p t n -> p (t n)"),
                                      maskT[:, :, :].rearrange("p t n -> p (t n)"),
                                      tm[g % TM_RING][:, :, :].rearrange("p t n -> p (t n)"),
                                      ALU.subtract).then_inc(st.N_ready.sem, 1)

                def combine(st, s, r, l, h, part):
                    F = D // HEADS[l]
                    done = st.head_steps
                    W = F + 1
                    q, num = st.q[:, :, 0:W], st.num[:, :, 0:W]
                    rr = st.r[:, :, h:h + 1].broadcast_to([P, NT, W])

                    def side(name, a, n):
                        return bank((name, s, l, h))[:, 0:NT * n * W].rearrange(
                            "p (t a f) -> p t a f", t=NT, a=n)[:, :, a, :]

                    if part:
                        dve.wait_ge(done.sem, done.upto(r, head_step(l, h, part)))
                    if l == 2 and part == 0:
                        dve.wait_ge(*is_ready(("T", s, l, h), r))
                        dve.wait_ge(st.vh_ready.sem, st.vh_ready.upto(r, NT))
                        ins = dve.tensor_tensor(q, st.vh[:, :, h * W:(h + 1) * W], side("T", 1, 2), ALU.subtract)
                    elif l == 2 and part == 1:
                        ins = dve.tensor_tensor(q, q, rr, ALU.mult)
                    elif part == 0:
                        dve.wait_ge(*is_ready(("N", s, l, h), r))
                        ins = dve.tensor_tensor(q, side("N", 0, 1), rr, ALU.mult)
                    elif part == (2 if l == 2 else 1):
                        ins = dve.tensor_tensor(num, side("T", 0, 2 if l == 2 else 1), q, ALU.add)
                    elif part == (3 if l == 2 else 2):
                        ins = dve.reciprocal(st.rec[:, :], st.num[:, :, F])
                    else:
                        ins = dve.tensor_tensor(st.hp[:, :, h * F:(h + 1) * F], st.num[:, :, 0:F],
                                                st.rec[:, :].unsqueeze(2).broadcast_to([P, NT, F]), ALU.mult)
                    ins.then_inc(done.sem, 1)

                def residual2(st, s, r, q):
                    dve.wait_ge(*is_ready(("wout", s, q), r))
                    dve.tensor_tensor(half(st.t, q), bank(("wout", s, q))[:, :], half(st.x, q),
                                      ALU.add).then_inc(st.t_ready.sem, 1)

                def low(st, s, r, l, q):
                    if q == 0:
                        dve.wait_ge(st.head_steps.sem, st.head_steps.upto(r, head_step(l, HEADS[l] - 1, 4)))
                    dve.tensor_scalar(half(st.eb, q), half(st.hp, q), 0.0, None, ALU.min).then_inc(
                        st.low_ready.sem, 1)

                def residual3(st, s, r, l, q):
                    y, e, n = half(st.hp, q), half(st.eb, q), ELU0[l] + q + 1
                    dve.wait_ge(st.elu1.sem, st.elu1.upto(r, n))
                    dve.scalar_tensor_tensor(out=y, in0=y, scalar=0.0, in1=e, op0=ALU.max,
                                             op1=ALU.add).then_inc(st.sum1.sem, 1)
                    dve.wait_ge(st.sum1.sem, st.sum1.upto(r, n))
                    dve.scalar_tensor_tensor(out=half(st.t, q), in0=y, scalar=-1.0, in1=half(st.x, q),
                                             op0=ALU.add, op1=ALU.add).then_inc(st.t_ready.sem, 1)

                return {"rows": rows, "score": score, "wide_weights": wide_weights, "den": den, "divide": divide,
                        "fold": fold, "divide1": divide1, "residual1": residual1, "stats": stats, "norm": norm,
                        "products": products, "T": T, "N": N, "combine": combine, "residual2": residual2,
                        "low": low, "residual3": residual3}

            whole_iteration(dve, "vector", steps_of)

        @block.scalar
        def _(act):
            act.wait_ge(const_made, N_CONST)
            act.wait_ge(setup_v, 3)
            act.activation(bt[:, 2:3], bt[:, 1:2], ACT.Exp, scale=-1.0).then_inc(setup_a, 1)
            act.wait_ge(setup_a, 1)
            act.activation(bt[:, 3:4], bt[:, 2:3], ACT.Ln, bias=plus_one[:, 0:1]).then_inc(setup_a, 1)
            act.wait_ge(setup_v, 4)
            act.activation(logs, logs, ACT.Ln, bias=eps_prior[:, 0:1]).then_inc(setup_a, 1)
            act.wait_ge(setup_v, 11)
            act.activation(logs, logs, ACT.Exp, scale=bt[:, 5:6]).then_inc(setup_a, 1)
            act.wait_ge(setup_v, V_SETUP)

            def steps_of(it):
                def copy(job, r, out, signal, n=NODES):
                    act.wait_ge(*is_ready(job, r))
                    act.activation(out, bank(job)[:, 0:n], ACT.Copy).then_inc(signal.sem, 1)

                def relu(job, r, out, signal, bias):
                    act.wait_ge(*is_ready(job, r))
                    act.activation(out, bank(job)[:, :], ACT.Relu, bias=bias).then_inc(signal.sem, 1)

                def xT(st, s, r, l):
                    for k in range(KD):
                        copy(("xT", s, l, k), r, st.xT[:, k, :], st.xT_ready)

                def oT(st, s, r):
                    for k in range(KD):
                        copy(("oT", s, 2, k), r, st.xT[:, k, :], st.xT_ready)

                def mlp1(st, s, r, c):
                    relu(("mlp1", s, c), r, st.oT[:, c, :], st.mlp1_ready, b1[:, c:c + 1])

                def mlp2(st, s, r, c):
                    relu(("mlp2", s, c), r, st.o3T[:, c, :], st.mlp2_ready, b2[:, c:c + 1])

                def h(st, s, r, l, t):
                    if l == 0:
                        copy(("h", s, 0, t, 0), r, st.h0[:, t, 0:D], st.h_ready, D)
                        copy(("h", s, 0, t, 1), r, st.h0[:, t, D:HID + 2], st.h_ready, HID + 2 - D)
                        return
                    out, n = (st.h1, D + 2) if l == 1 else (st.hf, D + 2 * HEADS[l])
                    copy(("h", s, l, t, 0), r, out[:, t, 0:n], st.h_ready, n)

                def exps(st, s, r, l):
                    H = HEADS[l]
                    F = D // H
                    act.wait_ge(st.col_steps.sem, st.col_steps.upto(r, COL0[l] + 2))
                    arg = st.u2[:, :, 0:H]
                    if l in WIDE:
                        u, v = st.u[:, :].unsqueeze(2), st.v[:, :].unsqueeze(2)
                    else:
                        u, v = (st.parts[l][0][:, :, :, a, F] for a in range(2))
                    act.activation(u, arg, ACT.Exp).then_inc(st.exp_ready.sem, 1)
                    act.activation(v, arg, ACT.Exp, scale=SLOPE).then_inc(st.exp_ready.sem, 1)
                    act.wait_ge(st.col_steps.sem, st.col_steps.upto(r, COL0[l] + (3 if l in WIDE else 5)))
                    z, out = (st.zb[:, :], st.rb[:, :]) if l in WIDE else (st.z[:, :, 0:H], st.r[:, :, 0:H])
                    act.activation(out, z, ACT.Exp, scale=SLOPE - 1.0).then_inc(st.exp_ready.sem, 1)

                def elu(st, s, r, l, k):
                    piece = half(st.eb, k % 2)
                    n = LOW0[l] + (2 * k + 2 if l == 1 else k + 1)
                    act.wait_ge(st.low_ready.sem, st.low_ready.upto(r, n))
                    act.activation(piece, piece, ACT.Exp).then_inc(st.elu1.sem, 1)
                    if l in WIDE:
                        act.wait_ge(st.elu1.sem, st.elu1.upto(r, ELU0[l] + k + 1))
                        act.activation(piece, piece, ACT.Exp, bias=neg_one[:, 0:1]).then_inc(st.elu2.sem, 1)

                def step(st, s, r, l, h):
                    g = FIRST_HEAD[l] + h
                    before = tenant_before(tm_before["T", s, l, h], it)
                    if before:
                        (_, *head), when = before
                        act.wait_ge(*is_ready(("T" if head[1] == 2 else "N", *head), when))
                    act.wait_ge(*is_ready(("f1", s, l, h), r))
                    if h == 0:
                        act.wait_ge(st.col_steps.sem, st.col_steps.upto(r, COL0[l] + 4))
                    for t in range(NT):
                        act.activation(tm[g % TM_RING][:, t, :], bank(("f1", s, l, h))[:, :], ACT.Relu,
                                       scale=STEEP, bias=st.steep[:, t, h:h + 1]).then_inc(st.step_ready.sem, 1)

                def all_v(st, s, r, t):
                    copy(("all_v", s, t), r, st.vh[:, t, :], st.vh_ready, 8 * 33)

                return {"xT": xT, "oT": oT, "mlp1": mlp1, "mlp2": mlp2, "h": h, "exps": exps, "elu": elu,
                        "step": step, "all_v": all_v}

            whole_iteration(act, "scalar", steps_of)

        @block.tensor
        def _(pe):
            pe.wait_ge(setup_v, V_TRANSPOSED["masks"])
            for n in range(2 * NT):
                src, j = (mask16, prior16)[n // NT], n % NT
                for t in range(NT):
                    last = pe.transpose(banks[n][:, :].bitcast(BF16)[:, t * P:(t + 1) * P],
                                        src[:, t, j * P:(j + 1) * P], ident16[:, :])
                last.then_inc(setup_t, 1)
            pe.wait_ge(setup_v, V_TRANSPOSED["banks"])
            for k in range(KD):
                for o in range(KD):
                    last = pe.transpose(banks[k][:, o * P:(o + 1) * P], wo_nat[:, o, k * P:(k + 1) * P], ident[:, :])
                last.then_inc(setup_t, 1)
            pe.wait_ge(setup_v, V_SETUP)

            def steps_of(it):
                def begin(job):
                    before = tenant_before(bank_before[job], it)
                    if before:
                        signal, n = emptied(before[0])
                        pe.wait_ge(signal.sem, signal.upto(before[1], n))
                    return bank(job)

                def end(job, last):
                    last.then_inc(S[job[1]].product_done.sem, 1)

                def transposes(job, src, pieces):
                    out = begin(job)
                    for n, (t, k) in enumerate(pieces):
                        last = pe.transpose(out[:, n * P:(n + 1) * P], src[:, t, k * P:(k + 1) * P], ident[:, :])
                    end(job, last)

                def products(job, K, lhsT, rhs, n, wait=None):
                    out = begin(job)
                    for k in range(K):
                        if wait:
                            wait(k)
                        last = pe.matmul(out[:, 0:n], lhsT(k), rhs(k), start=(k == 0), stop=(k == K - 1))
                    end(job, last)

                def node_tile(x, t):
                    return lambda k: x[:, k, t * P:(t + 1) * P]

                def xT(st, s, r, l):
                    if l == 0:
                        pe.wait_ge(st.x_loaded.sem, st.x_loaded.upto(r, 16))
                    else:
                        pe.wait_ge(st.norm_steps.sem, st.norm_steps.upto(r, NORM0[l - 1] + 14))
                    for k in range(KD):
                        transposes(("xT", s, l, k), st.x_in if l == 0 else st.x, [(t, k) for t in range(NT)])

                def mlp1(st, s, r, c):
                    products(("mlp1", s, c), KD, lambda k: w1[:, k, c * P:(c + 1) * P], lambda k: st.xT[:, k, :], NODES,
                             lambda k: c or pe.wait_ge(st.xT_ready.sem, st.xT_ready.upto(r, XT0[0] + k + 1)))

                def h(st, s, r, l, t):
                    if l == 0:
                        first = lambda k: t or pe.wait_ge(st.mlp1_ready.sem, st.mlp1_ready.upto(r, k + 1))
                        products(("h", s, 0, t, 0), KH, node_tile(st.oT, t), lambda k: wx[0][:, k, 0:D], D, first)
                        products(("h", s, 0, t, 1), KH, node_tile(st.oT, t), lambda k: wx[0][:, k, D:HID + 2],
                                 HID + 2 - D)
                    elif l == 1:
                        first = lambda k: t or pe.wait_ge(st.mlp2_ready.sem, st.mlp2_ready.upto(r, k + 1))
                        products(("h", s, 1, t, 0), KD, node_tile(st.o3T, t), lambda k: wx[1][:, k, :], D + 2, first)
                    else:
                        first = lambda k: t or pe.wait_ge(st.xT_ready.sem, st.xT_ready.upto(r, XT0[l] + k + 1))
                        products(("h", s, l, t, 0), KD, node_tile(st.xT, t), lambda k: wx[l][:, k, :],
                                 D + 2 * HEADS[l], first)

                def rows(st, s, r, l):
                    f = dict(zip(("f1_rows", "f2_rows"), score_columns(l, st)))
                    for name in ("f1_rows", "f2_rows"):
                        out = begin((name, s, l))
                        if name == "f1_rows":
                            pe.wait_ge(st.h_ready.sem, st.h_ready.upto(r, H0[l] + (8 if l == 0 else 4)))
                        for t in range(NT):
                            last = pe.transpose(out[0:HEADS[l], t * P:(t + 1) * P], f[name][:, t, :], ident[:, :])
                        end((name, s, l), last)

                def f1(st, s, r, l, h):
                    out = begin(("f1", s, l, h))
                    end(("f1", s, l, h), pe.matmul(out[:, :], sel[:, h, :], st.fr[:, :], start=True, stop=True))

                def score(st, s, r, l):
                    H = HEADS[l]
                    out = begin(("M", s, l))
                    pe.wait_ge(st.row_steps.sem, st.row_steps.upto(r, 4 * l + 4))
                    end(("M", s, l), pe.matmul(out[:, 0:H], ones[0:H, :], st.dg[0:H, 0:H], start=True, stop=True))
                    f1(st, s, r, l, 0)

                def den(st, s, r):
                    products(("den", s), NT, lambda k: ones[:, :], lambda k: st.pT[:, k, :], NODES,
                             lambda k: pe.wait_ge(st.pT_steps.sem, st.pT_steps.upto(r, k + 1)))

                def wide_out(st, s, r, l, n):
                    if l == 0:
                        products(("wide_out", s, 0, n), NT, lambda k: st.h0[:, k, n * P:(n + 1) * P],
                                 lambda k: st.pT[:, k, :], NODES)
                    else:
                        products(("wide_out", s, 1, n), NT, node_tile(st.pT, n), lambda k: st.h1[:, k, :], D + 3,
                                 lambda k: n or pe.wait_ge(st.pT_steps.sem, st.pT_steps.upto(r, 2 * NT + k + 1)))

                def mlp2(st, s, r, c):
                    products(("mlp2", s, c), KH, lambda k: w2[:, k, c * P:(c + 1) * P], lambda k: st.oT[:, k, :], NODES,
                             lambda k: c or pe.wait_ge(st.sum2.sem, st.sum2.upto(r, k + 1)))

                def res(st, s, r, q):
                    transposes(("res", s, q), st.o3T, [(k, t) for t in (2 * q, 2 * q + 1) for k in range(KD)])

                def heads(st, s, r, l, h):
                    g, W = FIRST_HEAD[l] + h, D // HEADS[l] + 1
                    sides = [("T", tm[g % TM_RING], slice(0, 2))] if l == 2 else [
                        ("T", tm[g % TM_RING], slice(0, 1)), ("N", nm[h % NM_RING], slice(1, 2))]
                    for name, w, a in sides:
                        out = begin((name, s, l, h))
                        if name == "T":
                            pe.wait_ge(st.T_ready.sem, st.T_ready.upto(r, g + 1))
                        else:
                            pe.wait_ge(st.N_ready.sem, st.N_ready.upto(r, g - 8 + 1))
                        n = W * (a.stop - a.start)
                        for t in range(NT):
                            for j in range(NT):
                                if h == 0 and t == 0 and name == "T":
                                    pe.wait_ge(st.rest2_ready.sem, st.rest2_ready.upto(r, R0[l] + j + 1))
                                for part in range(3):
                                    x = st.parts[l][part][:, j, h, a, :].rearrange("p a f -> p (a f)")
                                    last = pe.matmul(out[:, t * n:(t + 1) * n], w[:, j, t * P:(t + 1) * P],
                                                     x.bitcast(BF16)[:, 1::2], start=(j == 0 and part == 0),
                                                     stop=(j == NT - 1 and part == 2))
                        end((name, s, l, h), last)

                def all_v(st, s, r, t):
                    out = begin(("all_v", s, t))
                    n = 8 * 33
                    for j in range(NT):
                        pe.wait_ge(st.rest2_ready.sem, st.rest2_ready.upto(r, R0[2] + j + 1))
                        for part in range(3):
                            x = upper(st.parts[2][part], j).rearrange("p (h a f) -> p h a f", h=8, a=2)[:, :, 1, :]
                            last = pe.matmul(out[:, 0:n].rearrange("p (h f) -> p h f", h=8),
                                             priorT[:, j, t * P:(t + 1) * P], x, start=(j == 0 and part == 0),
                                             stop=(j == NT - 1 and part == 2))
                    end(("all_v", s, t), last)

                def oT(st, s, r):
                    pe.wait_ge(st.head_steps.sem, st.head_steps.upto(r, head_step(2, 7, 5)))
                    for k in range(KD):
                        transposes(("oT", s, 2, k), st.hp, [(t, k) for t in range(NT)])

                def wout(st, s, r, q):
                    out = begin(("wout", s, q))
                    if q == 0:
                        pe.wait_ge(st.xT_ready.sem, st.xT_ready.upto(r, XT0["oT"] + KD))
                    for n in range(2):
                        t = 2 * q + n
                        for k in range(KD):
                            last = pe.matmul(out[:, n * D:(n + 1) * D], st.xT[:, k, t * P:(t + 1) * P],
                                             woT[:, k, :], start=(k == 0), stop=(k == KD - 1))
                    end(("wout", s, q), last)

                return {"xT": xT, "mlp1": mlp1, "h": h, "rows": rows, "score": score, "f1": f1, "den": den,
                        "wide_out": wide_out, "mlp2": mlp2, "res": res, "heads": heads, "all_v": all_v,
                        "oT": oT, "wout": wout}

            whole_iteration(pe, "tensor", steps_of)


_INS = ["x", "adj", "L0_gnn_mlp1_w", "L0_gnn_mlp1_b", "L0_gnn_mlp2_w", "L0_gnn_mlp2_b", "L0_gnn_W_fc",
        "L0_gnn_a_fc", "L0_gnn_W_hand", "L0_gnn_a_hand", "L1_gnn_W", "L1_gnn_a_src", "L1_gnn_a_dst",
        "L1_gnn_beta_tilde", "L1_gnn_W_out", "L2_gnn_W", "L2_gnn_a", "L3_gnn_W", "L3_gnn_a"]


def kernel(**inputs):
    import concourse.bacc as bacc
    import numpy as np
    from concourse.bass_utils import run_bass_kernel_spmd

    nc = bacc.Bacc("TRN2", target_bir_lowering=False, num_devices=1)
    arrays, args = {}, []
    for name in _INS:
        a = np.ascontiguousarray(inputs[name])
        if a.ndim == 0:
            a = a.reshape(1)
        arrays[f"in_{name}_dram"] = a
        args.append(nc.dram_tensor(f"in_{name}_dram", a.shape, mybir.dt.from_np(a.dtype), kind="ExternalInput").ap())
    out = nc.dram_tensor("out_0_dram", inputs["x"].shape, mybir.dt.float32, kind="ExternalOutput").ap()
    build_program(nc, *args, out)
    r = run_bass_kernel_spmd(nc, [arrays], core_ids=[0])
    return r.results[0]["out_0_dram"]
```

```python
from contextlib import ExitStack

import concourse.bass as bass
from concourse import mybir

ALU = mybir.AluOpType
ACT = mybir.ActivationFunctionType
AX = mybir.AxisListType
F32 = mybir.dt.float32
F32R = mybir.dt.float32r
BF16 = mybir.dt.bfloat16
I32 = mybir.dt.int32

P = 128
STREAMS = 2
BANKS = 8
EPS_LN = 1e-5
EPS_PRIOR = 1e-6
SLOPE = 0.2
Z_MIN = -75.0
STEEP = 2.0 ** 100
STEPS_A_REGISTER = 16
V_SETUP = 45

HEADS = {0: 1, 1: 1, 2: 8, 3: 4, 4: 4}
WIDE = (0, 1)
MULTI = (2, 3, 4)
FIRST_HEAD = {2: 0, 3: 8, 4: 12}
TM_RING, NM_RING = 3, 2


SCHEDULE = {
    "tensor": """
        xT.0 ~h.2.1 ~h.2.2 ~h.2.3 mlp1.0 mlp1.1 ~rows.2 mlp1.2 mlp1.3 ~score.2 h.0.0 h.0.1 ~f1.2.1 ~f1.2.2
        ~f1.2.3 ~all_v.0 ~all_v.1 ~heads.2.0 ~all_v.2 ~all_v.3 ~heads.2.1 ~f1.2.4 ~f1.2.5 ~heads.2.2 ~f1.2.6
        ~heads.2.3 ~f1.2.7 h.0.2 ~heads.2.4 ~heads.2.5 ~heads.2.6 h.0.3 ~heads.2.7 rows.0 ~oT score.0 ~wout.0
        ~wout.1 den ~xT.3 ~h.3.0 ~h.3.1 ~h.3.2 ~h.3.3 ~rows.3 wide_out.0.0 ~score.3 wide_out.0.1 ~f1.3.1 ~f1.3.2
        wide_out.0.2 ~f1.3.3 ~heads.3.0 ~heads_n.3.0 wide_out.0.3 ~heads.3.1 ~heads_n.3.1 ~heads.3.2 ~heads.3.3
        ~heads_n.3.2 ~heads_n.3.3 mlp2.0 mlp2.1 h.1.0 h.1.1 h.1.2 h.1.3 rows.1 ~xT.4 score.1 ~h.4.0 ~h.4.1
        ~h.4.2 ~h.4.3 ~rows.4 wide_out.1.0 ~score.4 ~f1.4.1 wide_out.1.1 ~f1.4.2 wide_out.1.2 wide_out.1.3
        ~f1.4.3 res.0 ~heads.4.0 res.1 ~heads_n.4.0 ~heads_n.4.1 ~heads.4.1 ~heads.4.2 ~heads.4.3 ~heads_n.4.2
        xT.2 ~heads_n.4.3 h.2.0""",
    "vector": """
        ~rows.2.0 ~rows.2.1 ~rows.2.2 ~score.2.0 ~score.2.1 ~score.2.2 ~products.2.0 ~products.2.1 ~rest1.2.0
        ~rest1.2.1 ~products.2.2 ~rest1.2.2 ~products.2.3 ~rest1.2.3 ~T.2.0 ~T.2.1 ~T.2.2 ~T.2.3 ~combine.2.0.0
        ~combine.2.0.1 ~combine.2.0.2 ~combine.2.0.3 ~combine.2.0.4 ~combine.2.1.0 ~combine.2.1.1 ~combine.2.1.2
        ~combine.2.1.3 ~combine.2.1.4 ~combine.2.2.0 ~combine.2.2.1 ~combine.2.2.2 ~T.2.4 ~combine.2.2.3
        ~combine.2.2.4 ~combine.2.3.0 ~combine.2.3.1 ~T.2.5 ~T.2.6 ~combine.2.3.2 ~combine.2.3.3 ~combine.2.3.4
        ~combine.2.4.0 ~combine.2.4.1 ~combine.2.4.2 ~T.2.7 ~combine.2.4.3 ~combine.2.4.4 ~combine.2.5.0
        ~combine.2.5.1 ~combine.2.5.2 ~combine.2.5.3 ~combine.2.5.4 ~combine.2.6.0 ~combine.2.6.1 ~combine.2.6.2
        ~combine.2.6.3 ~combine.2.6.4 ~combine.2.7.0 ~combine.2.7.1 ~combine.2.7.2 ~combine.2.7.3 ~combine.2.7.4
        rows.0.0 rows.0.1 rows.0.2 score.0.0 score.0.1 wide_weights.0.0 wide_weights.0.1 ~residual2.0 ~stats.2.0
        ~residual2.1 ~stats.2.1 ~stats.2.2 ~stats.2.3 wide_weights.0.2 wide_weights.0.3 ~norm.2 den ~rows.3.0
        ~score.3.0 ~rows.3.1 ~rows.3.2 ~score.3.1 divide.0 ~products.3.0 ~score.3.2 ~products.3.1 ~rest1.3.0
        ~products.3.2 ~products.3.3 ~rest1.3.1 ~rest1.3.2 ~T.3.0 ~rest1.3.3 fold.0.0 ~N.3.0 fold.0.1 ~T.3.1
        divide.1 divide.2 ~combine.3.0.0 ~N.3.1 ~T.3.2 ~combine.3.0.1 ~T.3.3 fold.1.0 ~combine.3.0.2 ~N.3.2
        ~N.3.3 ~combine.3.0.3 ~combine.3.1.0 fold.1.1 ~combine.3.1.1 divide.3 ~combine.3.1.2 fold.2.0
        ~combine.3.1.3 ~combine.3.2.0 fold.2.1 ~combine.3.2.1 fold.3.0 ~combine.3.2.2 fold.3.1 ~combine.3.2.3
        ~combine.3.3.0 ~combine.3.3.1 ~combine.3.3.2 ~combine.3.3.3 ~residual3.3.0.0 ~residual3.3.1.0
        ~residual3.3.0.1 ~residual3.3.1.1 ~stats.3.0 ~stats.3.1 ~stats.3.2 ~stats.3.3 ~norm.3 rows.1.0 rows.1.1
        rows.1.2 score.1.0 score.1.1 wide_weights.1.0 wide_weights.1.1 wide_weights.1.2 wide_weights.1.3 mask.0
        mask.1 mask.2 mask.3 ~rows.4.0 ~score.4.0 ~rows.4.1 ~rows.4.2 ~score.4.1 divide1.0 ~score.4.2
        ~products.4.0 ~products.4.1 ~products.4.2 ~products.4.3 ~rest1.4.0 ~T.4.0 ~rest1.4.1 ~rest1.4.2
        divide1.1 ~T.4.1 divide1.2 divide1.3 ~rest1.4.3 ~N.4.0 ~N.4.1 residual1.0.0 residual1.1.0 ~T.4.2
        residual1.0.1 ~combine.4.0.0 residual1.1.1 residual1.0.2 residual1.1.2 ~combine.4.0.1 stats.1.0
        ~combine.4.0.2 stats.1.1 ~T.4.3 ~combine.4.0.3 stats.1.2 ~combine.4.1.0 stats.1.3 ~N.4.2 ~combine.4.1.1
        norm.1 ~combine.4.1.2 ~N.4.3 ~combine.4.1.3 ~combine.4.2.0 ~combine.4.2.1 ~combine.4.2.2 ~combine.4.2.3
        ~combine.4.3.0 ~combine.4.3.1 ~combine.4.3.2 ~combine.4.3.3 ~residual3.4.0.0 ~residual3.4.1.0
        ~residual3.4.0.1 ~residual3.4.1.1 ~stats.4.0 ~stats.4.1 ~stats.4.2 ~stats.4.3 ~norm.4""",
    "scalar": """
        xT.0 ~h.2.1 ~h.2.2 ~h.2.3 ~rows.2 mlp1.0 mlp1.1 mlp1.2 mlp1.3 ~exps.2 ~step.2.0 h.0.0 ~step.2.1 h.0.1
        ~all_v.0 ~step.2.2 ~step.2.3 ~all_v.1 ~all_v.2 ~all_v.3 ~step.2.4 ~step.2.5 ~step.2.6 ~step.2.7 h.0.2
        h.0.3 rows.0 ~oT exps.0 ~xT.3 ~h.3.0 ~h.3.1 ~h.3.2 ~h.3.3 ~rows.3 ~exps.3 ~step.3.0 elu.0.0 ~step.3.1
        ~step.3.2 ~step.3.3 elu.0.1 elu.0.2 elu.0.3 mlp2.0 ~elu.3.0 ~elu.3.1 mlp2.1 h.1.0 h.1.1 h.1.2 h.1.3
        rows.1 ~xT.4 exps.1 ~h.4.0 ~h.4.1 ~h.4.2 ~h.4.3 ~rows.4 ~exps.4 ~step.4.0 ~step.4.1 ~step.4.2 elu.1.0
        elu.1.1 ~step.4.3 xT.2 h.2.0 ~elu.4.0 ~elu.4.1""",
    "gpsimd": """
        ~rest2.2.0 ~rest2.2.1 ~rest2.2.2 ~rest2.2.3 ~rstd.2 ~rest2.3.0 ~rest2.3.1 ~rest2.3.2 ~rest2.3.3 ~rstd.3
        ~rest2.4.0 ~rest2.4.1 ~rest2.4.2 ~rest2.4.3 rstd.1 ~rstd.4""",
}


def timeline():
    steps = []
    for first in range(STREAMS):
        for engine, line in SCHEDULE.items():
            for word in line.split():
                step, *at = word.lstrip("~").split(".")
                s, behind = (1 - first, 1 - first) if word[0] == "~" else (first, 0)
                steps.append((s, behind, engine, step, tuple(int(x) for x in at)))
    return steps


def jobs_of(step, s, *at):
    if step == "xT":
        return [("xT", s, at[0], k) for k in range(2)]
    if step == "oT":
        return [("oT", s, 2, k) for k in range(2)]
    if step == "h":
        return [("h", s, *at, half) for half in range(2 if at[0] == 0 else 1)]
    if step == "rows":
        return [("rows", s, at[0])]
    if step == "score":
        return [("M", s, at[0]), ("f1", s, at[0], 0)]
    if step == "heads":
        return [("T", s, *at)]
    if step == "heads_n":
        return [("N", s, *at)]
    return [(step, s, *at)]


class Ahead:

    def __init__(self, value, by):
        self.value, self.by = value, by


class Signal:

    def __init__(self, ctx, nc, name, per):
        self.sem = ctx.enter_context(nc.semaphore(name))
        self.per = per

    def upto(self, r, k):
        it, behind = r if isinstance(r, tuple) else (r, 0)
        if isinstance(it, Ahead):
            it, behind = it.value, behind + it.by
        return it * self.per + (k - behind * self.per)


def build_program(nc, x_in, adj, mlp1_w, mlp1_b, mlp2_w, mlp2_b, W_fc, a_fc, W_hand, a_hand,
                  L1_W, L1_a_src, L1_a_dst, L1_beta, L1_W_out, L2_W, L2_a, L3_W, L3_a, y_out):
    B, NODES, D = x_in.shape
    HID = mlp1_w.shape[1]
    NT = NODES // P
    KD = D // P
    KH = HID // P
    ROUNDS = B // STREAMS
    assert NODES == 512 and D == 256 and HID == 512 and B % STREAMS == 0 and ROUNDS >= 3
    KIN = {0: KH, 1: KD, 2: KD, 3: KD, 4: KD}
    WIDTH = {0: HID, 1: D, 2: D, 3: D, 4: D}

    steps = timeline()

    body_jobs = [(job, behind) for s, behind, engine, step, at in steps if engine == "tensor"
                 for job in jobs_of(step, s, *at)]
    behind_of = dict(body_jobs)
    bank_of = {job: n % BANKS for n, (job, _) in enumerate(body_jobs)}
    number = {}
    for s in range(STREAMS):
        mine = [job for lag in (0, 1) for job, behind in body_jobs if job[1] == s and behind == lag]
        number.update({job: n for n, job in enumerate(mine)})
    jobs_per_round = len(number) // STREAMS

    def chain(users):
        return {job: (users[:n][::-1], users[-1]) for n, job in enumerate(users)}

    bank_before, tm_before, nm_before = {}, {}, {}
    for b in range(BANKS):
        bank_before.update(chain([job for job, _ in body_jobs if bank_of[job] == b]))
    for k in range(TM_RING):
        tm_before.update(chain([job for job, _ in body_jobs
                                if job[0] == "T" and (FIRST_HEAD[job[2]] + job[3]) % TM_RING == k]))
    for k in range(NM_RING):
        nm_before.update(chain([job for job, _ in body_jobs if job[0] == "N" and job[3] % NM_RING == k]))

    def tenant_before(before, it):
        same, last = before
        for job in same:
            if not isinstance(it, int) or behind_of[job] == (it == ROUNDS):
                return job, (it, behind_of[job])
        if isinstance(it, int) and it == 0:
            return None
        assert behind_of[last] == 0, "the first iteration doesn't have it"
        return last, (it, 1)

    with ExitStack() as ctx:
        def sb(name, shape, dt=F32):
            return ctx.enter_context(nc.sbuf_tensor(name, shape, dt))

        banks = [ctx.enter_context(nc.psum_tensor(f"bank{b}", [P, 512], F32)) for b in range(BANKS)]

        def bank(job):
            return banks[bank_of[job]]

        ident = sb("ident", [P, P])
        ident16 = sb("ident16", [P, P], BF16)
        ones = sb("ones", [P, P])
        sel = sb("sel", [64, 8, P], F32R)
        neg_one = sb("neg_one", [P, 1])
        plus_one = sb("plus_one", [P, 1])
        eps_prior = sb("eps_prior", [P, 1])
        minus_half = sb("minus_half", [P, NT])
        maskT = sb("maskT", [P, NT, NODES], BF16)
        priorT = sb("priorT", [P, NT, NODES], BF16)
        w1 = sb("w1", [P, KD, HID])
        b1 = sb("b1", [P, KH])
        w2 = sb("w2", [P, KH, D])
        b2 = sb("b2", [P, KD])
        woT = sb("woT", [P, KD, D])
        wx = {l: sb(f"wx{l}", [P, KIN[l], WIDTH[l] + 2 * HEADS[l]]) for l in HEADS}
        tm = [sb(f"tm{k}", [P, NT, NODES], BF16) for k in range(TM_RING)]
        nm = [sb(f"nm{k}", [P, NT, NODES], BF16) for k in range(NM_RING)]

        class Stream:
            pass

        S = []
        for s in range(STREAMS):
            st = Stream()
            st.x_in = sb(f"x_in{s}", [P, NT, D])
            st.x = sb(f"x{s}", [P, NT, D])
            st.t = sb(f"t{s}", [P, NT, D])
            st.xT = sb(f"xT{s}", [P, KD, NODES])
            st.region = region = sb(f"region{s}", [P, 3 * 8 * 2 * 33 * NT])
            wide = KH * NODES
            st.oT = region[:, 0:wide].rearrange("p (k n) -> p k n", k=KH)
            st.pT = region[:, wide:2 * wide].rearrange("p (k n) -> p k n", k=NT)
            st.h0 = region[:, 2 * wide:2 * wide + NT * (HID + 2)].rearrange("p (k n) -> p k n", k=NT)
            st.parts = {}
            for l in MULTI:
                H, F = HEADS[l], D // HEADS[l]
                n = NT * H * 2 * (F + 1)
                st.parts[l] = [region[:, k * n:(k + 1) * n].rearrange(
                    "p (t h a f) -> p t h a f", t=NT, h=H, a=2) for k in range(3)]
            st.h1 = sb(f"h1_{s}", [P, NT, D + 3])
            st.hf = sb(f"hf{s}", [P, NT, D + 16])
            st.o3T = sb(f"o3T{s}", [P, KD, NODES])
            st.zb = st.rb = st.rden = sb(f"zb{s}", [P, NODES])
            st.hp = sb(f"hp{s}", [P, NT, D])
            st.eb = sb(f"eb{s}", [P, NT, D])
            st.vh = sb(f"vh{s}", [P, NT, 8 * 33])
            st.fr = sb(f"fr{s}", [64, NODES], F32R)
            st.mx = sb(f"mx{s}", [16, 1])
            st.dg = sb(f"dg{s}", [16, 8])
            st.M = sb(f"M{s}", [P, 8])
            st.u2 = sb(f"u2_{s}", [P, NT, 8])
            st.z = sb(f"z{s}", [P, NT, 8])
            st.steep = sb(f"steep{s}", [P, NT, 8])
            st.u = sb(f"u{s}", [P, NT])
            st.v = sb(f"v{s}", [P, NT])
            st.r = sb(f"r{s}", [P, NT, 8])
            st.q = sb(f"q{s}", [P, NT, 65])
            st.num = sb(f"num{s}", [P, NT, 65])
            st.rec = sb(f"rec{s}", [P, NT])
            st.bn = sb(f"bn{s}", [P, NT, 6])
            st.mv = sb(f"mv{s}", [P, NT, 2])
            st.ve = sb(f"ve{s}", [P, NT])
            st.rstd = sb(f"rstd{s}", [P, NT])

            def signal(name, per, s=s):
                return Signal(ctx, nc, f"{name}{s}", per)

            st.x_loaded = signal("x_loaded", 16)
            st.x_in_used = signal("x_in_used", 2)
            st.y_stored = signal("y_stored", 16)
            st.product_done = signal("product_done", jobs_per_round)
            st.xT_ready = signal("xT_ready", 10)
            st.mlp1_ready = signal("mlp1_ready", 4)
            st.mlp2_ready = signal("mlp2_ready", 2)
            st.h_ready = signal("h_ready", 24)
            st.exp_ready = signal("exp_ready", 15)
            st.f_rounded = signal("f_rounded", 5)
            st.below_ready = signal("below_ready", 10)
            st.elu1 = signal("elu1_", 10)
            st.elu2 = signal("elu2_", 6)
            st.step_ready = signal("step_ready", 64)
            st.vh_ready = signal("vh_ready", 4)
            st.row_steps = signal("row_steps", 15)
            st.col_steps = signal("col_steps", 18)
            st.pT_steps = signal("pT_steps", 8)
            st.masked = signal("masked", 4)
            st.rden_ready = signal("rden_ready", 1)
            st.y_steps = signal("y_steps", 12)
            st.sum1 = signal("sum1_", 10)
            st.sum2 = signal("sum2_", 6)
            st.t_ready = signal("t_ready", 6)
            st.T_ready = signal("T_ready", 16)
            st.N_ready = signal("N_ready", 8)
            st.head_steps = signal("head_steps", 8 * 5 + 8 * 4)
            st.product_ready = signal("product_ready", 24)
            st.rest1_ready = signal("rest1_ready", 12)
            st.norm_steps = signal("norm_steps", 4 * 14)
            st.rest2_ready = signal("rest2_ready", 12)
            st.rstd_ready = signal("rstd_ready", 4)
            S.append(st)

        XT0 = {0: 0, 2: 2, "oT": 4, 3: 6, 4: 8}
        H0 = {0: 0, 1: 8, 2: 12, 3: 16, 4: 20}
        COL0 = {0: 0, 1: 3, 2: 6, 3: 10, 4: 14}
        ELU0 = {0: 0, 1: 4, 3: 6, 4: 8}
        NORM0 = {1: 0, 2: 14, 3: 28, 4: 42}
        T0 = {2: 0, 3: 2, 4: 4}
        X0 = {2: 0, 3: 8, 4: 16}
        R0 = {2: 0, 3: 4, 4: 8}

        def head_step(l, h, k):
            return 5 * h + k if l == 2 else 40 + 4 * (FIRST_HEAD[l] - 8 + h) + k

        def is_ready(job, r):
            done = S[job[1]].product_done
            return done.sem, done.upto(r, number[job] + 1)

        def emptied(job):
            name, s, *at = job
            st = S[s]
            l = at[0] if at else None
            if name == "xT":
                return st.xT_ready, XT0[l] + at[1] + 1
            if name == "oT":
                return st.xT_ready, XT0["oT"] + at[1] + 1
            if name == "mlp1":
                return st.mlp1_ready, at[0] + 1
            if name == "mlp2":
                return st.mlp2_ready, at[0] + 1
            if name == "rows":
                return st.row_steps, 3 * l + 3
            if name == "h":
                return st.h_ready, H0[l] + (2 * at[1] + at[2] if l == 0 else at[1]) + 1
            if name == "M":
                return st.col_steps, COL0[l] + (1 if l in WIDE else 3)
            if name == "f1":
                return (st.col_steps, COL0[l] + 3) if l in WIDE else (st.step_ready, 4 * (FIRST_HEAD[l] + at[1] + 1))
            if name == "den":
                return st.rden_ready, 1
            if name == "wide_out":
                return st.y_steps, at[1] + 1 if l == 0 else KH + 2 * at[1] + 2
            if name == "res":
                return st.sum2, KH + at[0] + 1
            if name == "all_v":
                return st.vh_ready, at[0] + 1
            if name == "N":
                return st.head_steps, head_step(*at, 1)
            if name == "T":
                return st.head_steps, head_step(*at, 3 if l == 2 else 2)
            assert name == "wout"
            return st.t_ready, T0[2] + at[0] + 1

        def half(x, q):
            return x[:, 2 * q:2 * q + 2, :].rearrange("p t d -> p (t d)")

        def flat(x, t):
            return x[:, t].rearrange("p h a f -> p (h a f)")

        def upper(x, t):
            return flat(x, t).bitcast(BF16)[:, 1::2]

        def score_columns(l, st):
            x = {0: st.h0, 1: st.h1}.get(l, st.hf)
            N, H = WIDTH[l], HEADS[l]
            return x[:, :, N:N + H], x[:, :, N + H:N + 2 * H]

        def whole_iteration(engine, name, steps_of):
            mine = [(s, behind, step, at) for s, behind, e, step, at in steps if e == name]

            def run(it, lags):
                now = it
                for n, (s, behind, step, at) in enumerate(mine):
                    if n % STEPS_A_REGISTER == 0 and not isinstance(it, int):
                        by = n // STEPS_A_REGISTER + 1
                        now = Ahead(engine.snap(it + by), by)
                    if behind in lags:
                        steps_of(now)[step](S[s], s, (now, behind), *at)

            run(0, (0,))
            with engine.Fori(1, ROUNDS) as it:
                run(it, (0, 1))
            run(ROUNDS, (1,))

        n_adj = NT * NODES
        adj_int = S[0].region[:, 0:n_adj].bitcast(I32)
        logs = S[0].region[:, n_adj:2 * n_adj]
        maskf = S[0].region[:, 2 * n_adj:3 * n_adj]
        logs_t = logs.rearrange("p (t n) -> p t n", t=NT)
        mask16, prior16 = tm[0], nm[0]
        wo_nat = S[1].hp
        sel_f = S[0].eb[0:64, :, :].rearrange("p t d -> p (t d)").rearrange("p (h n) -> p h n", h=8)
        bt = S[1].M
        rowmax = S[1].rec
        att_vec, off = {}, 0
        for l in HEADS:
            for part in range(2):
                att_vec[l, part] = S[1].region[:, off:off + WIDTH[l]]
                off += WIDTH[l]
        prod = S[1].region[:, off:off + KH * HID]

        loads = ctx.enter_context(nc.semaphore("setup_loads"))
        const_made = ctx.enter_context(nc.semaphore("const_made"))
        setup_v = ctx.enter_context(nc.semaphore("setup_vector"))
        setup_a = ctx.enter_context(nc.semaphore("setup_scalar"))
        setup_t = ctx.enter_context(nc.semaphore("setup_tensor"))
        N_LOADS = 4 + 2 * KD + 1 + 6 + 2 + 8 + 5
        N_CONST = 10 + 2 * STREAMS
        V_TRANSPOSED = {}

        block = ctx.enter_context(nc.Block())

        @block.sync
        def _(sp):
            n_loads = [0]

            def load(dst, src, **kw):
                sp.dma_start(dst, src, **kw).then_inc(loads, 16)
                n_loads[0] += 1

            load(adj_int.rearrange("p (t n) -> p t n", t=NT), adj.rearrange("(t p) n -> p t n", p=P))
            load(bt[:, 0:1], L1_beta.partition_broadcast(P))
            load(wx[0][:, :, 0:HID], W_fc.rearrange("(k p) n -> p k n", p=P))
            load(wx[1][:, :, 0:D], W_hand.rearrange("(k p) n -> p k n", p=P))
            for l, w in ((2, L1_W), (3, L2_W)):
                for k in range(KD):
                    load(wx[l][:, k, 0:D].rearrange("p (h f) -> p h f", h=HEADS[l]),
                         w[:, k * P:(k + 1) * P, :].rearrange("h p f -> p h f"))
            load(wx[4][:, :, 0:D], L3_W.rearrange("(k p) n -> p k n", p=P))
            for part in range(2):
                F = D // 4
                load(att_vec[0, part], a_fc[part * HID:(part + 1) * HID, 0].partition_broadcast(P))
                load(att_vec[1, part], a_hand[part * D:(part + 1) * D, 0].partition_broadcast(P))
                load(att_vec[2, part], (L1_a_src, L1_a_dst)[part].rearrange("h f -> (h f)").partition_broadcast(P))
                load(att_vec[3, part].rearrange("p (h f) -> p h f", h=4),
                     L2_a[:, part * F:(part + 1) * F].partition_broadcast(P))
                for h in range(4):
                    load(att_vec[4, part][:, h * F:(h + 1) * F],
                         L3_a[part * F:(part + 1) * F].partition_broadcast(P))
            load(w1[:, :, :], mlp1_w.rearrange("(k p) n -> p k n", p=P))
            load(w2[:, :, :], mlp2_w.rearrange("(k p) n -> p k n", p=P))
            load(wo_nat[:, 0:KD, :], L1_W_out.rearrange("(k p) n -> p k n", p=P))
            load(b1[:, :], mlp1_b.rearrange("(k p) -> p k", p=P), allow_slow_non_contiguous=True)
            load(b2[:, :], mlp2_b.rearrange("(k p) -> p k", p=P), allow_slow_non_contiguous=True)
            assert n_loads[0] == N_LOADS

            def load_x(s, r):
                st = S[s]
                sp.dma_start(st.x_in[:, :, :], x_in[bass.ds(r * STREAMS + s, 1), :, :].rearrange(
                    "o (t p) d -> p (o t) d", p=P)).then_inc(st.x_loaded.sem, 16)

            def next_x(s, r):
                sp.wait_ge(S[s].x_in_used.sem, S[s].x_in_used.upto(r, 2))
                load_x(s, r + 1)

            def store_y(s, r):
                st = S[s]
                sp.wait_ge(st.norm_steps.sem, st.norm_steps.upto(r, NORM0[4] + 14))
                sp.dma_start(y_out[bass.ds(r * STREAMS + s, 1), :, :].rearrange(
                    "o (t p) d -> p (o t) d", p=P), st.t[:, :, :]).then_inc(st.y_stored.sem, 16)

            for s in range(STREAMS):
                load_x(s, 0)
            next_x(0, 0)
            store_y(0, 0)
            next_x(1, 0)
            with sp.Fori(1, ROUNDS - 1) as it:
                store_y(1, it - 1)
                next_x(0, it)
                store_y(0, it)
                next_x(1, it)
            store_y(1, ROUNDS - 2)
            store_y(0, ROUNDS - 1)
            store_y(1, ROUNDS - 1)
            for st in S:
                sp.wait_ge(st.y_stored.sem, 16 * ROUNDS)

        @block.gpsimd
        def _(gp):
            gp.memset(ident[:, :], 0.0).then_inc(const_made, 1)
            gp.memset(sel_f[:, :, :], 0.0).then_inc(const_made, 1)
            gp.wait_ge(const_made, 2)
            gp.affine_select(out=ident[:, :], in_=ident[:, :], compare_op=ALU.not_equal, fill=1.0, base=0,
                             pattern=[[-1, P]], channel_multiplier=1).then_inc(const_made, 1)
            gp.affine_select(out=sel_f[:, :, :], in_=sel_f[:, :, :], compare_op=ALU.not_equal, fill=1.0,
                             base=0, pattern=[[-1, 8], [0, P]], channel_multiplier=1).then_inc(const_made, 1)
            gp.wait_ge(const_made, 4)
            gp.affine_select(out=sel_f[:, :, :], in_=sel_f[:, :, :], compare_op=ALU.not_equal, fill=1.0,
                             base=-32, pattern=[[-1, 8], [0, P]], channel_multiplier=1).then_inc(const_made, 1)
            gp.memset(ones[:, :], 1.0).then_inc(const_made, 1)
            gp.memset(neg_one[:, :], -1.0).then_inc(const_made, 1)
            gp.memset(plus_one[:, :], 1.0).then_inc(const_made, 1)
            gp.memset(eps_prior[:, :], EPS_PRIOR).then_inc(const_made, 1)
            gp.memset(minus_half[:, :], -0.5).then_inc(const_made, 1)
            for st in S:
                gp.memset(st.fr[:, :].bitcast(F32), 0.0).then_inc(const_made, 1)
                gp.memset(st.h1[:, :, D + 2:D + 3], 1.0).then_inc(const_made, 1)
            gp.wait_ge(setup_v, V_SETUP)

            def steps_of(it):
                def rstd(st, s, r, l):
                    gp.wait_ge(st.norm_steps.sem, st.norm_steps.upto(r, NORM0[l] + 10))
                    gp.tensor_tensor(st.rstd[:, :], st.ve[:, :], minus_half[:, :], ALU.pow).then_inc(
                        st.rstd_ready.sem, 1)

                def rest2(st, s, r, l, t):
                    x0, x1, x2 = st.parts[l]
                    gp.wait_ge(st.rest1_ready.sem, st.rest1_ready.upto(r, R0[l] + t + 1))
                    gp.tensor_tensor(flat(x2, t), flat(x1, t), upper(x1, t), ALU.subtract).then_inc(
                        st.rest2_ready.sem, 1)

                return {"rstd": rstd, "rest2": rest2}

            whole_iteration(gp, "gpsimd", steps_of)

        @block.vector
        def _(dve):
            done = [0]

            def step(ins, wait=True):
                ins.then_inc(setup_v, 1)
                done[0] += 1
                if wait:
                    dve.wait_ge(setup_v, done[0])

            dve.wait_ge(loads, 16 * N_LOADS)
            step(dve.tensor_scalar(bt[:, 1:2], bt[:, 0:1], -1.0, None, ALU.mult))
            step(dve.tensor_tensor(bt[:, 1:2], bt[:, 0:1], bt[:, 1:2], ALU.max))
            step(dve.tensor_scalar(bt[:, 6:7], bt[:, 0:1], 0.0, None, ALU.max), False)
            step(dve.tensor_scalar(logs, adj_int, 0.0, None, ALU.max), False)
            step(dve.tensor_scalar(maskf, adj_int, 0.0, None, ALU.is_gt))
            dve.wait_ge(setup_a, 3)
            step(dve.tensor_reduce(rowmax[:, :], logs_t, AX.X, ALU.max))
            for t in range(NT):
                step(dve.tensor_scalar(logs_t[:, t, :], logs_t[:, t, :], rowmax[:, t:t + 1], None, ALU.subtract))
            step(dve.tensor_tensor(bt[:, 5:6], bt[:, 6:7], bt[:, 3:4], ALU.add))
            assert done[0] == 11
            dve.wait_ge(const_made, N_CONST)
            step(dve.tensor_copy(mask16[:, :, :].rearrange("p t n -> p (t n)"), maskf))
            dve.wait_ge(setup_a, 4)
            step(dve.tensor_tensor(prior16[:, :, :].rearrange("p t n -> p (t n)"), logs, maskf, ALU.mult))
            step(dve.tensor_copy(ident16[:, :], ident[:, :]))
            V_TRANSPOSED["masks"] = done[0]
            step(dve.tensor_copy(sel[:, :, :], sel_f[:, :, :]))
            for l in HEADS:
                H, K, N = HEADS[l], KIN[l], WIDTH[l]
                for part in range(2):
                    step(dve.tensor_tensor(prod[:, 0:K * N].rearrange("p (k n) -> p k n", k=K), wx[l][:, :, 0:N],
                                           att_vec[l, part].unsqueeze(1).broadcast_to([P, K, N]), ALU.mult))
                    step(dve.tensor_reduce(wx[l][:, :, N + part * H:N + (part + 1) * H],
                                           prod[:, 0:K * N].rearrange("p (k h f) -> p k h f", k=K, h=H),
                                           AX.X, ALU.add))
            for n in range(2 * NT):
                dve.wait_ge(setup_t, n + 1)
                step(dve.tensor_copy((maskT, priorT)[n // NT][:, n % NT, :],
                                     banks[n][:, :].bitcast(BF16)[:, 0:NODES]), False)
            V_TRANSPOSED["banks"] = done[0]
            for k in range(KD):
                dve.wait_ge(setup_t, 2 * NT + k + 1)
                step(dve.tensor_copy(woT[:, k, :], banks[k][:, 0:D]), False)
            dve.wait_ge(setup_v, done[0])
            assert done[0] == V_SETUP, done[0]

            def steps_of(it):
                def rows(st, s, r, l, part):
                    H, done, n = HEADS[l], st.row_steps, 3 * l
                    f = bank(("rows", s, l))[0:2 * H, :]
                    if part == 0:
                        dve.wait_ge(st.f_rounded.sem, st.f_rounded.upto(r, l + 1))
                        ins = dve.tensor_reduce(st.mx[0:2 * H, :], f, AX.X, ALU.max)
                    elif part == 1:
                        dve.wait_ge(done.sem, done.upto(r, n + 1))
                        ins = dve.tensor_scalar(st.dg[0:2 * H, 0:H], ident[0:2 * H, H:2 * H], st.mx[0:2 * H, 0:1],
                                                None, ALU.mult)
                    else:
                        ins = dve.tensor_tensor(st.fr[32:32 + 2 * H, :], f, st.fr[0:2 * H, :].bitcast(F32),
                                                ALU.subtract)
                    ins.then_inc(done.sem, 1)

                def score(st, s, r, l, part):
                    H, done, n = HEADS[l], st.col_steps, COL0[l]
                    f1, f2 = score_columns(l, st)
                    if l in WIDE:
                        if part == 0:
                            dve.wait_ge(*is_ready(("M", s, l), r))
                            dve.tensor_copy(st.M[:, 0:1], bank(("M", s, l))[:, 0:1]).then_inc(done.sem, 1)
                            return
                        dve.wait_ge(done.sem, done.upto(r, n + 1))
                        M = st.M[:, 0:1].unsqueeze(1).broadcast_to([P, NT, 1])
                        dve.tensor_tensor(st.u2[:, :, 0:1], f2, M, ALU.subtract).then_inc(done.sem, 1)
                        dve.wait_ge(*is_ready(("f1", s, l, 0), r))
                        dve.tensor_scalar(st.zb[:, :], bank(("f1", s, l, 0))[:, :], st.M[:, 0:1], Z_MIN,
                                          ALU.add, ALU.max).then_inc(done.sem, 1)
                        return
                    if part == 0:
                        dve.wait_ge(st.h_ready.sem, st.h_ready.upto(r, H0[l] + 4))
                        dve.tensor_scalar(st.steep[:, :, 0:H], f2, STEEP, None, ALU.mult).then_inc(done.sem, 1)
                    elif part == 1:
                        dve.wait_ge(*is_ready(("M", s, l), r))
                        M = bank(("M", s, l))[:, 0:H].unsqueeze(1).broadcast_to([P, NT, H])
                        dve.tensor_tensor(st.u2[:, :, 0:H], f2, M, ALU.subtract).then_inc(done.sem, 1)
                        dve.tensor_tensor(st.z[:, :, 0:H], f1, M, ALU.add).then_inc(done.sem, 1)
                    else:
                        dve.wait_ge(done.sem, done.upto(r, n + 3))
                        dve.tensor_scalar(st.z[:, :, 0:H], st.z[:, :, 0:H], Z_MIN, None, ALU.max).then_inc(done.sem, 1)

                def wide_weights(st, s, r, l, t):
                    if t == 0:
                        dve.wait_ge(st.exp_ready.sem, st.exp_ready.upto(r, 3 * l + 3))
                    dve.tensor_scalar(st.pT[:, t, :], st.rb[:, :], st.v[:, t:t + 1], st.u[:, t:t + 1],
                                      ALU.mult, ALU.max).then_inc(st.pT_steps.sem, 1)

                def mask(st, s, r, t):
                    dve.wait_ge(st.pT_steps.sem, st.pT_steps.upto(r, NT + t + 1))
                    dve.tensor_tensor(st.pT[:, t, :], st.pT[:, t, :], maskT[:, t, :],
                                      ALU.mult).then_inc(st.masked.sem, 1)

                def den(st, s, r):
                    dve.wait_ge(*is_ready(("den", s), r))
                    dve.reciprocal(st.rden[:, :], bank(("den", s))[:, :]).then_inc(st.rden_ready.sem, 1)

                def divide(st, s, r, c):
                    out = bank(("wide_out", s, 0, c))
                    dve.wait_ge(*is_ready(("wide_out", s, 0, c), r))
                    if c == 0:
                        dve.wait_ge(st.rden_ready.sem, st.rden_ready.upto(r, 1))
                    if c >= 2:
                        dve.wait_ge(st.sum2.sem, st.sum2.upto(r, c - 1))
                    dve.tensor_tensor(half(st.hp, c % 2), out[:, :], st.rden[:, :], ALU.mult).then_inc(
                        st.y_steps.sem, 1)

                def fold(st, s, r, c, part):
                    y, e, o = half(st.hp, c % 2), half(st.eb, c % 2), st.oT[:, c, :]
                    if part == 0:
                        dve.wait_ge(st.elu2.sem, st.elu2.upto(r, c + 1))
                        dve.scalar_tensor_tensor(out=e, in0=e, scalar=-1.0, in1=o, op0=ALU.add,
                                                 op1=ALU.add).then_inc(st.sum1.sem, 1)
                    else:
                        dve.wait_ge(st.sum1.sem, st.sum1.upto(r, c + 1))
                        dve.scalar_tensor_tensor(out=o, in0=y, scalar=0.0, in1=e, op0=ALU.max,
                                                 op1=ALU.add).then_inc(st.sum2.sem, 1)

                def divide1(st, s, r, t):
                    out = bank(("wide_out", s, 1, t))
                    dve.wait_ge(*is_ready(("wide_out", s, 1, t), r))
                    dve.reciprocal(st.rec[:, t:t + 1], out[:, D + 2:D + 3]).then_inc(st.y_steps.sem, 1)
                    dve.wait_ge(st.y_steps.sem, st.y_steps.upto(r, KH + 2 * t + 1))
                    dve.tensor_scalar(st.hp[:, t, :], out[:, 0:D], st.rec[:, t:t + 1], None,
                                      ALU.mult).then_inc(st.y_steps.sem, 1)

                def residual1(st, s, r, q, part):
                    y, e = half(st.hp, q), half(st.eb, q)
                    if part == 0:
                        dve.wait_ge(st.elu2.sem, st.elu2.upto(r, KH + q + 1))
                        dve.scalar_tensor_tensor(out=y, in0=y, scalar=0.0, in1=e, op0=ALU.max,
                                                 op1=ALU.add).then_inc(st.sum1.sem, 1)
                    elif part == 1:
                        dve.wait_ge(st.sum1.sem, st.sum1.upto(r, KH + q + 1))
                        dve.wait_ge(*is_ready(("res", s, q), r))
                        dve.scalar_tensor_tensor(out=y, in0=y, scalar=-1.0, in1=bank(("res", s, q))[:, :],
                                                 op0=ALU.add, op1=ALU.add).then_inc(st.sum2.sem, 1)
                    else:
                        dve.wait_ge(st.sum2.sem, st.sum2.upto(r, KH + q + 1))
                        if q == 0:
                            dve.wait_ge(st.x_loaded.sem, st.x_loaded.upto(r, 16))
                            dve.wait_ge(st.y_stored.sem, st.y_stored.upto(r, 0))
                        dve.scalar_tensor_tensor(out=half(st.t, q), in0=y, scalar=0.0, in1=half(st.x_in, q),
                                                 op0=ALU.max, op1=ALU.add).then_inc(st.x_in_used.sem, 1)

                def stats(st, s, r, l, part):
                    done, n = st.norm_steps, NORM0[l]
                    if part < 2:
                        if l == 1:
                            dve.wait_ge(st.x_in_used.sem, st.x_in_used.upto(r, part + 1))
                        else:
                            dve.wait_ge(st.t_ready.sem, st.t_ready.upto(r, T0[l] + part + 1))
                        for t in (2 * part, 2 * part + 1):
                            dve.bn_stats(st.bn[:, t, :], st.t[:, t, :]).then_inc(done.sem, 1)
                    elif part == 2:
                        dve.wait_ge(done.sem, done.upto(r, n + NT))
                        dve.memset(st.ve[:, :], EPS_LN).then_inc(done.sem, 1)
                        for t in range(NT):
                            dve.bn_aggr(st.mv[:, t, :], st.bn[:, t, :]).then_inc(done.sem, 1)
                    else:
                        dve.wait_ge(done.sem, done.upto(r, n + 9))
                        dve.tensor_tensor(st.ve[:, :], st.mv[:, :, 1], st.ve[:, :], ALU.add).then_inc(done.sem, 1)

                def norm(st, s, r, l):
                    dve.wait_ge(st.rstd_ready.sem, st.rstd_ready.upto(r, l))
                    out = st.t if l == 4 else st.x
                    for t in range(NT):
                        dve.tensor_scalar(out[:, t, :], st.t[:, t, :], st.mv[:, t, 0:1], st.rstd[:, t:t + 1],
                                          ALU.subtract, ALU.mult).then_inc(st.norm_steps.sem, 1)

                def products(st, s, r, l, t):
                    H = HEADS[l]
                    F = D // H
                    x0, h = st.parts[l][0], st.hf[:, t, 0:D].rearrange("p (h f) -> p h f", h=H)
                    if t == 0:
                        dve.wait_ge(st.exp_ready.sem, st.exp_ready.upto(r, 3 * l + 2))
                    for a in range(2):
                        dve.tensor_tensor(x0[:, t, :, a, 0:F], h, x0[:, t, :, a, F:F + 1].broadcast_to([P, H, F]),
                                          ALU.mult).then_inc(st.product_ready.sem, 1)

                def rest1(st, s, r, l, t):
                    x0, x1, _ = st.parts[l]
                    dve.wait_ge(st.product_ready.sem, st.product_ready.upto(r, X0[l] + 2 * t + 2))
                    dve.tensor_tensor(flat(x1, t), flat(x0, t), upper(x0, t), ALU.subtract).then_inc(
                        st.rest1_ready.sem, 1)

                def T(st, s, r, l, h):
                    g = FIRST_HEAD[l] + h
                    x = tm[g % TM_RING][:, :, :].rearrange("p t n -> p (t n)")
                    mask = (priorT if l == 2 else maskT)[:, :, :].rearrange("p t n -> p (t n)")
                    dve.wait_ge(st.step_ready.sem, st.step_ready.upto(r, 4 * g + 4))
                    dve.tensor_tensor(x, x, mask, ALU.min).then_inc(st.T_ready.sem, 1)

                def N(st, s, r, l, h):
                    g = FIRST_HEAD[l] + h
                    before = tenant_before(nm_before["N", s, l, h], it)
                    if before:
                        dve.wait_ge(*is_ready(*before))
                    dve.wait_ge(st.T_ready.sem, st.T_ready.upto(r, g + 1))
                    dve.tensor_tensor(nm[h % NM_RING][:, :, :].rearrange("p t n -> p (t n)"),
                                      maskT[:, :, :].rearrange("p t n -> p (t n)"),
                                      tm[g % TM_RING][:, :, :].rearrange("p t n -> p (t n)"),
                                      ALU.subtract).then_inc(st.N_ready.sem, 1)

                def combine(st, s, r, l, h, part):
                    F = D // HEADS[l]
                    done = st.head_steps
                    W = F + 1
                    q, num = st.q[:, :, 0:W], st.num[:, :, 0:W]
                    rr = st.r[:, :, h:h + 1].broadcast_to([P, NT, W])

                    def side(name, a, n):
                        return bank((name, s, l, h))[:, 0:NT * n * W].rearrange(
                            "p (t a f) -> p t a f", t=NT, a=n)[:, :, a, :]

                    if part:
                        dve.wait_ge(done.sem, done.upto(r, head_step(l, h, part)))
                    if l == 2 and part == 0:
                        dve.wait_ge(*is_ready(("T", s, l, h), r))
                        dve.wait_ge(st.vh_ready.sem, st.vh_ready.upto(r, NT))
                        ins = dve.tensor_tensor(q, st.vh[:, :, h * W:(h + 1) * W], side("T", 1, 2), ALU.subtract)
                    elif l == 2 and part == 1:
                        ins = dve.tensor_tensor(q, q, rr, ALU.mult)
                    elif part == 0:
                        dve.wait_ge(*is_ready(("N", s, l, h), r))
                        ins = dve.tensor_tensor(q, side("N", 0, 1), rr, ALU.mult)
                    elif part == (2 if l == 2 else 1):
                        dve.wait_ge(*is_ready(("T", s, l, h), r))
                        ins = dve.tensor_tensor(num, side("T", 0, 2 if l == 2 else 1), q, ALU.add)
                    elif part == (3 if l == 2 else 2):
                        ins = dve.reciprocal(st.rec[:, :], st.num[:, :, F])
                    else:
                        ins = dve.tensor_tensor(st.hp[:, :, h * F:(h + 1) * F], st.num[:, :, 0:F],
                                                st.rec[:, :].unsqueeze(2).broadcast_to([P, NT, F]), ALU.mult)
                    ins.then_inc(done.sem, 1)

                def residual2(st, s, r, q):
                    dve.wait_ge(*is_ready(("wout", s, q), r))
                    dve.tensor_tensor(half(st.t, q), bank(("wout", s, q))[:, :], half(st.x, q),
                                      ALU.add).then_inc(st.t_ready.sem, 1)

                def residual3(st, s, r, l, q, part):
                    y, e, n = half(st.hp, q), half(st.eb, q), ELU0[l] + q + 1
                    if part == 0:
                        dve.wait_ge(st.elu1.sem, st.elu1.upto(r, n))
                        dve.scalar_tensor_tensor(out=y, in0=y, scalar=0.0, in1=e, op0=ALU.max,
                                                 op1=ALU.add).then_inc(st.sum1.sem, 1)
                    else:
                        dve.wait_ge(st.sum1.sem, st.sum1.upto(r, n))
                        dve.scalar_tensor_tensor(out=half(st.t, q), in0=y, scalar=-1.0, in1=half(st.x, q),
                                                 op0=ALU.add, op1=ALU.add).then_inc(st.t_ready.sem, 1)

                return {"rows": rows, "score": score, "wide_weights": wide_weights, "den": den, "divide": divide,
                        "fold": fold, "divide1": divide1, "residual1": residual1, "stats": stats, "norm": norm,
                        "products": products, "T": T, "N": N, "combine": combine, "residual2": residual2,
                        "mask": mask, "rest1": rest1, "residual3": residual3}

            whole_iteration(dve, "vector", steps_of)

        @block.scalar
        def _(act):
            act.wait_ge(const_made, N_CONST)
            act.wait_ge(setup_v, 3)
            act.activation(bt[:, 2:3], bt[:, 1:2], ACT.Exp, scale=-1.0).then_inc(setup_a, 1)
            act.wait_ge(setup_a, 1)
            act.activation(bt[:, 3:4], bt[:, 2:3], ACT.Ln, bias=plus_one[:, 0:1]).then_inc(setup_a, 1)
            act.wait_ge(setup_v, 4)
            act.activation(logs, logs, ACT.Ln, bias=eps_prior[:, 0:1]).then_inc(setup_a, 1)
            act.wait_ge(setup_v, 11)
            act.activation(logs, logs, ACT.Exp, scale=bt[:, 5:6]).then_inc(setup_a, 1)
            act.wait_ge(setup_v, V_SETUP)

            def steps_of(it):
                def copy(job, r, out, signal, n=NODES):
                    act.wait_ge(*is_ready(job, r))
                    act.activation(out, bank(job)[:, 0:n], ACT.Copy).then_inc(signal.sem, 1)

                def relu(job, r, out, signal, bias):
                    act.wait_ge(*is_ready(job, r))
                    act.activation(out, bank(job)[:, :], ACT.Relu, bias=bias).then_inc(signal.sem, 1)

                def xT(st, s, r, l):
                    for k in range(KD):
                        copy(("xT", s, l, k), r, st.xT[:, k, :], st.xT_ready)

                def oT(st, s, r):
                    for k in range(KD):
                        copy(("oT", s, 2, k), r, st.xT[:, k, :], st.xT_ready)

                def mlp1(st, s, r, c):
                    relu(("mlp1", s, c), r, st.oT[:, c, :], st.mlp1_ready, b1[:, c:c + 1])

                def mlp2(st, s, r, c):
                    relu(("mlp2", s, c), r, st.o3T[:, c, :], st.mlp2_ready, b2[:, c:c + 1])

                def h(st, s, r, l, t):
                    if l == 0:
                        copy(("h", s, 0, t, 0), r, st.h0[:, t, 0:D], st.h_ready, D)
                        copy(("h", s, 0, t, 1), r, st.h0[:, t, D:HID + 2], st.h_ready, HID + 2 - D)
                        return
                    out, n = (st.h1, D + 2) if l == 1 else (st.hf, D + 2 * HEADS[l])
                    copy(("h", s, l, t, 0), r, out[:, t, 0:n], st.h_ready, n)

                def rows(st, s, r, l):
                    act.wait_ge(*is_ready(("rows", s, l), r))
                    act.activation(st.fr[0:2 * HEADS[l], :], bank(("rows", s, l))[0:2 * HEADS[l], :],
                                   ACT.Copy).then_inc(st.f_rounded.sem, 1)

                def exps(st, s, r, l):
                    H = HEADS[l]
                    F = D // H
                    act.wait_ge(st.col_steps.sem, st.col_steps.upto(r, COL0[l] + 2))
                    arg = st.u2[:, :, 0:H]
                    if l in WIDE:
                        u, v = st.u[:, :].unsqueeze(2), st.v[:, :].unsqueeze(2)
                    else:
                        u, v = (st.parts[l][0][:, :, :, a, F] for a in range(2))
                    act.activation(u, arg, ACT.Exp).then_inc(st.exp_ready.sem, 1)
                    act.activation(v, arg, ACT.Exp, scale=SLOPE).then_inc(st.exp_ready.sem, 1)
                    act.wait_ge(st.col_steps.sem, st.col_steps.upto(r, COL0[l] + (3 if l in WIDE else 4)))
                    z, out = (st.zb[:, :], st.rb[:, :]) if l in WIDE else (st.z[:, :, 0:H], st.r[:, :, 0:H])
                    act.activation(out, z, ACT.Exp, scale=SLOPE - 1.0).then_inc(st.exp_ready.sem, 1)

                def elu(st, s, r, l, k):
                    y, piece, n = half(st.hp, k % 2), half(st.eb, k % 2), ELU0[l] + k + 1
                    if l in WIDE:
                        act.wait_ge(st.y_steps.sem, st.y_steps.upto(r, k + 1 if l == 0 else KH + 4 * k + 4))
                    elif k == 0:
                        act.wait_ge(st.head_steps.sem, st.head_steps.upto(r, head_step(l, HEADS[l] - 1, 4)))
                    act.activation(piece, y, ACT.Relu, scale=-1.0).then_inc(st.below_ready.sem, 1)
                    act.wait_ge(st.below_ready.sem, st.below_ready.upto(r, n))
                    act.activation(piece, piece, ACT.Exp, scale=-1.0).then_inc(st.elu1.sem, 1)
                    if l in WIDE:
                        act.wait_ge(st.elu1.sem, st.elu1.upto(r, n))
                        act.activation(piece, piece, ACT.Exp, bias=neg_one[:, 0:1]).then_inc(st.elu2.sem, 1)

                def step(st, s, r, l, h):
                    g = FIRST_HEAD[l] + h
                    before = tenant_before(tm_before["T", s, l, h], it)
                    if before:
                        (_, its, layer, head), when = before
                        act.wait_ge(*is_ready(("T", its, layer, head), when))
                        if layer != 2:
                            act.wait_ge(S[its].N_ready.sem, S[its].N_ready.upto(
                                when, FIRST_HEAD[layer] + head - 8 + 1))
                    act.wait_ge(*is_ready(("f1", s, l, h), r))
                    if h == 0:
                        act.wait_ge(st.col_steps.sem, st.col_steps.upto(r, COL0[l] + 1))
                    for t in range(NT):
                        act.activation(tm[g % TM_RING][:, t, :], bank(("f1", s, l, h))[:, :], ACT.Relu,
                                       scale=STEEP, bias=st.steep[:, t, h:h + 1]).then_inc(st.step_ready.sem, 1)

                def all_v(st, s, r, t):
                    copy(("all_v", s, t), r, st.vh[:, t, :], st.vh_ready, 8 * 33)

                return {"xT": xT, "oT": oT, "mlp1": mlp1, "mlp2": mlp2, "h": h, "rows": rows, "exps": exps,
                        "elu": elu, "step": step, "all_v": all_v}

            whole_iteration(act, "scalar", steps_of)

        @block.tensor
        def _(pe):
            pe.wait_ge(setup_v, V_TRANSPOSED["masks"])
            for n in range(2 * NT):
                src, j = (mask16, prior16)[n // NT], n % NT
                for t in range(NT):
                    last = pe.transpose(banks[n][:, :].bitcast(BF16)[:, t * P:(t + 1) * P],
                                        src[:, t, j * P:(j + 1) * P], ident16[:, :])
                last.then_inc(setup_t, 1)
            pe.wait_ge(setup_v, V_TRANSPOSED["banks"])
            for k in range(KD):
                for o in range(KD):
                    last = pe.transpose(banks[k][:, o * P:(o + 1) * P], wo_nat[:, o, k * P:(k + 1) * P], ident[:, :])
                last.then_inc(setup_t, 1)
            pe.wait_ge(setup_v, V_SETUP)

            def steps_of(it):
                def begin(job):
                    before = tenant_before(bank_before[job], it)
                    if before:
                        signal, n = emptied(before[0])
                        pe.wait_ge(signal.sem, signal.upto(before[1], n))
                    return bank(job)

                def end(job, last):
                    last.then_inc(S[job[1]].product_done.sem, 1)

                def transposes(job, src, pieces):
                    out = begin(job)
                    for n, (t, k) in enumerate(pieces):
                        last = pe.transpose(out[:, n * P:(n + 1) * P], src[:, t, k * P:(k + 1) * P], ident[:, :])
                    end(job, last)

                def products(job, K, lhsT, rhs, n, wait=None):
                    out = begin(job)
                    for k in range(K):
                        if wait:
                            wait(k)
                        last = pe.matmul(out[:, 0:n], lhsT(k), rhs(k), start=(k == 0), stop=(k == K - 1))
                    end(job, last)

                def node_tile(x, t):
                    return lambda k: x[:, k, t * P:(t + 1) * P]

                def xT(st, s, r, l):
                    if l == 0:
                        pe.wait_ge(st.x_loaded.sem, st.x_loaded.upto(r, 16))
                    else:
                        pe.wait_ge(st.norm_steps.sem, st.norm_steps.upto(r, NORM0[l - 1] + 14))
                    for k in range(KD):
                        transposes(("xT", s, l, k), st.x_in if l == 0 else st.x, [(t, k) for t in range(NT)])

                def mlp1(st, s, r, c):
                    products(("mlp1", s, c), KD, lambda k: w1[:, k, c * P:(c + 1) * P], lambda k: st.xT[:, k, :], NODES,
                             lambda k: c or pe.wait_ge(st.xT_ready.sem, st.xT_ready.upto(r, XT0[0] + k + 1)))

                def h(st, s, r, l, t):
                    if l == 0:
                        first = lambda k: t or pe.wait_ge(st.mlp1_ready.sem, st.mlp1_ready.upto(r, k + 1))
                        products(("h", s, 0, t, 0), KH, node_tile(st.oT, t), lambda k: wx[0][:, k, 0:D], D, first)
                        products(("h", s, 0, t, 1), KH, node_tile(st.oT, t), lambda k: wx[0][:, k, D:HID + 2],
                                 HID + 2 - D)
                    elif l == 1:
                        first = lambda k: t or pe.wait_ge(st.mlp2_ready.sem, st.mlp2_ready.upto(r, k + 1))
                        products(("h", s, 1, t, 0), KD, node_tile(st.o3T, t), lambda k: wx[1][:, k, :], D + 2, first)
                    else:
                        first = lambda k: t or pe.wait_ge(st.xT_ready.sem, st.xT_ready.upto(r, XT0[l] + k + 1))
                        products(("h", s, l, t, 0), KD, node_tile(st.xT, t), lambda k: wx[l][:, k, :],
                                 D + 2 * HEADS[l], first)

                def rows(st, s, r, l):
                    N, H, x = WIDTH[l], HEADS[l], {0: st.h0, 1: st.h1}.get(l, st.hf)
                    out = begin(("rows", s, l))
                    pe.wait_ge(st.h_ready.sem, st.h_ready.upto(r, H0[l] + (8 if l == 0 else 4)))
                    for t in range(NT):
                        last = pe.transpose(out[0:2 * H, t * P:(t + 1) * P], x[:, t, N:N + 2 * H], ident[:, :])
                    end(("rows", s, l), last)

                def f1(st, s, r, l, h):
                    out = begin(("f1", s, l, h))
                    end(("f1", s, l, h), pe.matmul(out[:, :], sel[:, h, :], st.fr[:, :], start=True, stop=True))

                def score(st, s, r, l):
                    H = HEADS[l]
                    out = begin(("M", s, l))
                    pe.wait_ge(st.row_steps.sem, st.row_steps.upto(r, 3 * l + 2))
                    end(("M", s, l), pe.matmul(out[:, 0:H], ones[0:2 * H, :], st.dg[0:2 * H, 0:H],
                                               start=True, stop=True))
                    pe.wait_ge(st.row_steps.sem, st.row_steps.upto(r, 3 * l + 3))
                    f1(st, s, r, l, 0)

                def den(st, s, r):
                    products(("den", s), NT, lambda k: ones[:, :], lambda k: st.pT[:, k, :], NODES,
                             lambda k: pe.wait_ge(st.pT_steps.sem, st.pT_steps.upto(r, k + 1)))

                def wide_out(st, s, r, l, n):
                    if l == 0:
                        products(("wide_out", s, 0, n), NT, lambda k: st.h0[:, k, n * P:(n + 1) * P],
                                 lambda k: st.pT[:, k, :], NODES)
                    else:
                        products(("wide_out", s, 1, n), NT, node_tile(st.pT, n), lambda k: st.h1[:, k, :], D + 3,
                                 lambda k: n or pe.wait_ge(st.masked.sem, st.masked.upto(r, k + 1)))

                def mlp2(st, s, r, c):
                    products(("mlp2", s, c), KH, lambda k: w2[:, k, c * P:(c + 1) * P], lambda k: st.oT[:, k, :], NODES,
                             lambda k: c or pe.wait_ge(st.sum2.sem, st.sum2.upto(r, k + 1)))

                def res(st, s, r, q):
                    transposes(("res", s, q), st.o3T, [(k, t) for t in (2 * q, 2 * q + 1) for k in range(KD)])

                def head_product(st, s, r, name, l, h, w, a):
                    n = (D // HEADS[l] + 1) * (a.stop - a.start)
                    out = begin((name, s, l, h))
                    for t in range(NT):
                        for j in range(NT):
                            if h == 0 and t == 0:
                                pe.wait_ge(st.rest2_ready.sem, st.rest2_ready.upto(r, R0[l] + j + 1))
                            for part in range(3):
                                x = st.parts[l][part][:, j, h, a, :].rearrange("p a f -> p (a f)")
                                last = pe.matmul(out[:, t * n:(t + 1) * n], w[:, j, t * P:(t + 1) * P],
                                                 x.bitcast(BF16)[:, 1::2], start=(j == 0 and part == 0),
                                                 stop=(j == NT - 1 and part == 2))
                    end((name, s, l, h), last)

                def heads(st, s, r, l, h):
                    g = FIRST_HEAD[l] + h
                    pe.wait_ge(st.T_ready.sem, st.T_ready.upto(r, g + 1))
                    head_product(st, s, r, "T", l, h, tm[g % TM_RING], slice(0, 2 if l == 2 else 1))

                def heads_n(st, s, r, l, h):
                    pe.wait_ge(st.N_ready.sem, st.N_ready.upto(r, FIRST_HEAD[l] + h - 8 + 1))
                    head_product(st, s, r, "N", l, h, nm[h % NM_RING], slice(1, 2))

                def all_v(st, s, r, t):
                    out = begin(("all_v", s, t))
                    n = 8 * 33
                    for j in range(NT):
                        pe.wait_ge(st.rest2_ready.sem, st.rest2_ready.upto(r, R0[2] + j + 1))
                        for part in range(3):
                            x = upper(st.parts[2][part], j).rearrange("p (h a f) -> p h a f", h=8, a=2)[:, :, 1, :]
                            last = pe.matmul(out[:, 0:n].rearrange("p (h f) -> p h f", h=8),
                                             priorT[:, j, t * P:(t + 1) * P], x, start=(j == 0 and part == 0),
                                             stop=(j == NT - 1 and part == 2))
                    end(("all_v", s, t), last)

                def oT(st, s, r):
                    pe.wait_ge(st.head_steps.sem, st.head_steps.upto(r, head_step(2, 7, 5)))
                    for k in range(KD):
                        transposes(("oT", s, 2, k), st.hp, [(t, k) for t in range(NT)])

                def wout(st, s, r, q):
                    out = begin(("wout", s, q))
                    if q == 0:
                        pe.wait_ge(st.xT_ready.sem, st.xT_ready.upto(r, XT0["oT"] + KD))
                    for n in range(2):
                        t = 2 * q + n
                        for k in range(KD):
                            last = pe.matmul(out[:, n * D:(n + 1) * D], st.xT[:, k, t * P:(t + 1) * P],
                                             woT[:, k, :], start=(k == 0), stop=(k == KD - 1))
                    end(("wout", s, q), last)

                return {"xT": xT, "mlp1": mlp1, "h": h, "rows": rows, "score": score, "f1": f1, "den": den,
                        "wide_out": wide_out, "mlp2": mlp2, "res": res, "heads": heads, "heads_n": heads_n, "all_v": all_v,
                        "oT": oT, "wout": wout}

            whole_iteration(pe, "tensor", steps_of)


_INS = ["x", "adj", "L0_gnn_mlp1_w", "L0_gnn_mlp1_b", "L0_gnn_mlp2_w", "L0_gnn_mlp2_b", "L0_gnn_W_fc",
        "L0_gnn_a_fc", "L0_gnn_W_hand", "L0_gnn_a_hand", "L1_gnn_W", "L1_gnn_a_src", "L1_gnn_a_dst",
        "L1_gnn_beta_tilde", "L1_gnn_W_out", "L2_gnn_W", "L2_gnn_a", "L3_gnn_W", "L3_gnn_a"]


def kernel(**inputs):
    import concourse.bacc as bacc
    import numpy as np
    from concourse.bass_utils import run_bass_kernel_spmd

    nc = bacc.Bacc("TRN2", target_bir_lowering=False, num_devices=1)
    arrays, args = {}, []
    for name in _INS:
        a = np.ascontiguousarray(inputs[name])
        if a.ndim == 0:
            a = a.reshape(1)
        arrays[f"in_{name}_dram"] = a
        args.append(nc.dram_tensor(f"in_{name}_dram", a.shape, mybir.dt.from_np(a.dtype), kind="ExternalInput").ap())
    out = nc.dram_tensor("out_0_dram", inputs["x"].shape, mybir.dt.float32, kind="ExternalOutput").ap()
    build_program(nc, *args, out)
    r = run_bass_kernel_spmd(nc, [arrays], core_ids=[0])
    return r.results[0]["out_0_dram"]
```
